# Optimizing a Trainium2 kernel written in Bass

```python
import numpy as np
import jax
import jax.numpy as jnp

def _softmax(x, axis=-1):
    return jax.nn.softmax(x, axis=axis)

def _gelu(x):
    return jax.nn.gelu(x, approximate=True)

def _silu(x):
    return jax.nn.silu(x)

def _sigmoid(x):
    return jax.nn.sigmoid(x)

def _layernorm(x, axis=-1, eps=1e-05):
    m = jnp.mean(x, axis=axis, keepdims=True)
    v = jnp.var(x, axis=axis, keepdims=True)
    return (x - m) / jnp.sqrt(v + eps)

def _scatter_add(tgt, idx, src, axis=0):
    return tgt.at[idx].add(src)

def _segment_sum(src, seg, n):
    return jax.ops.segment_sum(src, seg, n)
kernel_name = 'mk_conv_seq_d2_conv_nchw128_r4_8f1e76'

def setup_inputs(seed: int=0):
    np.random.seed(seed)
    _w = jnp.asarray

    def _rec_inputs():
        import jax
        import jax.numpy as jnp
        _gk = jax.random.key(seed)
        x = -0.0003929 + 0.9999 * jax.random.normal(jax.random.fold_in(_gk, 1), (8, 32, 32, 32), jnp.float32)
        return x
    x = _rec_inputs()

    def _L0_conv_setup():
        import jax, jax.numpy as jnp
        import numpy as np
        B, C, H, W = (8, 32, 32, 32)
        HEADS = 8
        E = 2
        EC = C * E
        EPS = 1e-05

        def _conv(x, w, pad):
            return jax.lax.conv_general_dilated(x, w, window_strides=(1, 1), padding=[(pad, pad), (pad, pad)], dimension_numbers=('NCHW', 'OIHW', 'NCHW'))

        def _ln_last(x, g, b):
            m = jnp.mean(x, axis=-1, keepdims=True)
            v = jnp.mean((x - m) ** 2, axis=-1, keepdims=True)
            return (x - m) / jnp.sqrt(v + EPS) * g + b
        key = jax.random.key(seed)
        ks = jax.random.split(key, 14)

        def w(k, shape):
            return jax.random.normal(k, shape, dtype=jnp.float32) * 0.02
        return {'x': jax.random.normal(ks[0], (B, C, H, W), dtype=jnp.float32), 'ln1_g': jnp.ones((C,), jnp.float32), 'ln1_b': jnp.zeros((C,), jnp.float32), 'scale': jnp.ones((1,), jnp.float32), 'q1': w(ks[1], (C, C, 1, 1)), 'q3': w(ks[2], (C, C, 3, 3)), 'k1': w(ks[3], (C, C, 1, 1)), 'k3': w(ks[4], (C, C, 3, 3)), 'v1': w(ks[5], (C, C, 1, 1)), 'v3': w(ks[6], (C, C, 3, 3)), 'o_w': w(ks[7], (C, C, 1, 1)), 'ln2_g': jnp.ones((C,), jnp.float32), 'ln2_b': jnp.zeros((C,), jnp.float32), 'g1': w(ks[8], (EC, C, 1, 1)), 'g3': w(ks[9], (EC, EC, 3, 3)), 'i1': w(ks[10], (EC, C, 1, 1)), 'i3': w(ks[11], (EC, EC, 3, 3)), 'r1': w(ks[12], (C, EC, 1, 1))}
    _L0_conv_all = _L0_conv_setup()
    _L0_conv_in = {k: v for k, v in _L0_conv_all.items() if k in ('ln1_g', 'ln1_b', 'scale', 'q1', 'q3', 'k1', 'k3', 'v1', 'v3', 'o_w', 'ln2_g', 'ln2_b', 'g1', 'g3', 'i1', 'i3', 'r1')}
    del _L0_conv_all

    def _L1_conv_setup():
        import jax, jax.numpy as jnp
        import numpy as np
        KERNEL = 3
        PAD = 1
        EPS = 1e-05
        NEG_SLOPE = 0.2

        def conv2d(x, w, b, pad):
            y = jax.lax.conv_general_dilated(x, w, window_strides=(1, 1), padding=[(pad, pad), (pad, pad)], dimension_numbers=('NCHW', 'OIHW', 'NCHW'))
            return y + b[None, :, None, None]

        def _refine(x, conv2_w, conv2_b, mask_w, mask_b, q_w, q_b, k_w, k_b, v_w, v_b):
            B, C, H, W = x.shape
            out1 = conv2d(x, conv2_w, conv2_b, PAD)
            mask = jax.nn.sigmoid(conv2d(x, mask_w, mask_b, PAD))
            xm = x * mask
            q = conv2d(xm, q_w, q_b, 0)
            pad_x = jnp.pad(xm, ((0, 0), (0, 0), (PAD, PAD), (PAD, PAD)))
            k = conv2d(pad_x, k_w, k_b, 0)
            v = conv2d(pad_x, v_w, v_b, 0)
            sims = [jnp.sum(q * k[:, :, i:i + H, j:j + W], axis=1) for i in range(KERNEL) for j in range(KERNEL)]
            attn = jax.nn.softmax(jnp.stack(sims, axis=-1), axis=-1)
            out2 = jnp.zeros_like(out1)
            idx = 0
            for i in range(KERNEL):
                for j in range(KERNEL):
                    out2 = out2 + attn[..., idx][:, None] * v[:, :, i:i + H, j:j + W]
                    idx += 1
            return out1 * mask + (1.0 - mask) * out2
        key = jax.random.key(seed)
        ks = jax.random.split(key, 14)
        C = 32
        B, H, W = (8, 32, 32)
        w3 = lambda k: jax.random.normal(k, (C, C, 3, 3), dtype=jnp.float32) * 0.05
        w1 = lambda k: jax.random.normal(k, (C, C, 1, 1), dtype=jnp.float32) * 0.05
        bz = lambda k: jax.random.normal(k, (C,), dtype=jnp.float32) * 0.01
        return {'x': jax.random.normal(ks[0], (B, C, H, W), dtype=jnp.float32), 'conv1_w': w3(ks[1]), 'conv1_b': bz(ks[2]), 'conv2_w': w3(ks[3]), 'conv2_b': bz(ks[4]), 'mask_w': w3(ks[5]), 'mask_b': bz(ks[6]), 'q_w': w1(ks[7]), 'q_b': bz(ks[8]), 'k_w': w1(ks[9]), 'k_b': bz(ks[10]), 'v_w': w1(ks[11]), 'v_b': bz(ks[12])}
    _L1_conv_all = _L1_conv_setup()
    _L1_conv_in = {k: v for k, v in _L1_conv_all.items() if k in ('conv1_w', 'conv1_b', 'conv2_w', 'conv2_b', 'mask_w', 'mask_b', 'q_w', 'q_b', 'k_w', 'k_b', 'v_w', 'v_b')}
    del _L1_conv_all
    return {'x': x, 'L0_conv_ln1_g': _L0_conv_in['ln1_g'], 'L0_conv_ln1_b': _L0_conv_in['ln1_b'], 'L0_conv_scale': _L0_conv_in['scale'], 'L0_conv_q1': _L0_conv_in['q1'], 'L0_conv_q3': _L0_conv_in['q3'], 'L0_conv_k1': _L0_conv_in['k1'], 'L0_conv_k3': _L0_conv_in['k3'], 'L0_conv_v1': _L0_conv_in['v1'], 'L0_conv_v3': _L0_conv_in['v3'], 'L0_conv_o_w': _L0_conv_in['o_w'], 'L0_conv_ln2_g': _L0_conv_in['ln2_g'], 'L0_conv_ln2_b': _L0_conv_in['ln2_b'], 'L0_conv_g1': _L0_conv_in['g1'], 'L0_conv_g3': _L0_conv_in['g3'], 'L0_conv_i1': _L0_conv_in['i1'], 'L0_conv_i3': _L0_conv_in['i3'], 'L0_conv_r1': _L0_conv_in['r1'], 'L1_conv_conv1_w': _L1_conv_in['conv1_w'], 'L1_conv_conv1_b': _L1_conv_in['conv1_b'], 'L1_conv_conv2_w': _L1_conv_in['conv2_w'], 'L1_conv_conv2_b': _L1_conv_in['conv2_b'], 'L1_conv_mask_w': _L1_conv_in['mask_w'], 'L1_conv_mask_b': _L1_conv_in['mask_b'], 'L1_conv_q_w': _L1_conv_in['q_w'], 'L1_conv_q_b': _L1_conv_in['q_b'], 'L1_conv_k_w': _L1_conv_in['k_w'], 'L1_conv_k_b': _L1_conv_in['k_b'], 'L1_conv_v_w': _L1_conv_in['v_w'], 'L1_conv_v_b': _L1_conv_in['v_b']}

def reference(x, L0_conv_ln1_g, L0_conv_ln1_b, L0_conv_scale, L0_conv_q1, L0_conv_q3, L0_conv_k1, L0_conv_k3, L0_conv_v1, L0_conv_v3, L0_conv_o_w, L0_conv_ln2_g, L0_conv_ln2_b, L0_conv_g1, L0_conv_g3, L0_conv_i1, L0_conv_i3, L0_conv_r1, L1_conv_conv1_w, L1_conv_conv1_b, L1_conv_conv2_w, L1_conv_conv2_b, L1_conv_mask_w, L1_conv_mask_b, L1_conv_q_w, L1_conv_q_b, L1_conv_k_w, L1_conv_k_b, L1_conv_v_w, L1_conv_v_b):
    import jax
    import jax.numpy as jnp

    def _L0_conv_ref(x, ln1_g, ln1_b, scale, q1, q3, k1, k3, v1, v3, o_w, ln2_g, ln2_b, g1, g3, i1, i3, r1):
        import jax, jax.numpy as jnp
        import numpy as np
        B, C, H, W = (8, 32, 32, 32)
        HEADS = 8
        E = 2
        EC = C * E
        EPS = 1e-05

        def _conv(x, w, pad):
            return jax.lax.conv_general_dilated(x, w, window_strides=(1, 1), padding=[(pad, pad), (pad, pad)], dimension_numbers=('NCHW', 'OIHW', 'NCHW'))

        def _ln_last(x, g, b):
            m = jnp.mean(x, axis=-1, keepdims=True)
            v = jnp.mean((x - m) ** 2, axis=-1, keepdims=True)
            return (x - m) / jnp.sqrt(v + EPS) * g + b
        d = C // HEADS
        HW = H * W
        xn = _ln_last(x, ln1_g, ln1_b)
        q = _conv(_conv(xn, q1, 0), q3, 1).reshape(B, HEADS, HW, d)
        k = _conv(_conv(xn, k1, 0), k3, 1).reshape(B, HEADS, HW, d)
        v = _conv(_conv(xn, v1, 0), v3, 1).reshape(B, HEADS, HW, d)
        score = jnp.einsum('bhpd,bhpe->bhde', k, q) / scale
        probs = jax.nn.softmax(score, axis=-1)
        attn = jnp.einsum('bhpd,bhde->bhpe', v, probs)
        attn = attn.transpose(0, 1, 3, 2).reshape(B, C, H, W)
        x = _conv(attn, o_w, 0) + x
        xn = _ln_last(x, ln2_g, ln2_b)
        gate = jax.nn.gelu(_conv(_conv(xn, g1, 0), g3, 1), approximate=False)
        info = _conv(_conv(xn, i1, 0), i3, 1)
        out = _conv(gate * info, r1, 0) + x
        return out

    def _L1_conv_ref(x, conv1_w, conv1_b, conv2_w, conv2_b, mask_w, mask_b, q_w, q_b, k_w, k_b, v_w, v_b):
        import jax, jax.numpy as jnp
        import numpy as np
        KERNEL = 3
        PAD = 1
        EPS = 1e-05
        NEG_SLOPE = 0.2

        def conv2d(x, w, b, pad):
            y = jax.lax.conv_general_dilated(x, w, window_strides=(1, 1), padding=[(pad, pad), (pad, pad)], dimension_numbers=('NCHW', 'OIHW', 'NCHW'))
            return y + b[None, :, None, None]

        def _refine(x, conv2_w, conv2_b, mask_w, mask_b, q_w, q_b, k_w, k_b, v_w, v_b):
            B, C, H, W = x.shape
            out1 = conv2d(x, conv2_w, conv2_b, PAD)
            mask = jax.nn.sigmoid(conv2d(x, mask_w, mask_b, PAD))
            xm = x * mask
            q = conv2d(xm, q_w, q_b, 0)
            pad_x = jnp.pad(xm, ((0, 0), (0, 0), (PAD, PAD), (PAD, PAD)))
            k = conv2d(pad_x, k_w, k_b, 0)
            v = conv2d(pad_x, v_w, v_b, 0)
            sims = [jnp.sum(q * k[:, :, i:i + H, j:j + W], axis=1) for i in range(KERNEL) for j in range(KERNEL)]
            attn = jax.nn.softmax(jnp.stack(sims, axis=-1), axis=-1)
            out2 = jnp.zeros_like(out1)
            idx = 0
            for i in range(KERNEL):
                for j in range(KERNEL):
                    out2 = out2 + attn[..., idx][:, None] * v[:, :, i:i + H, j:j + W]
                    idx += 1
            return out1 * mask + (1.0 - mask) * out2
        residual = x
        out = conv2d(x, conv1_w, conv1_b, PAD)
        mu = jnp.mean(out, axis=(2, 3), keepdims=True)
        var = jnp.var(out, axis=(2, 3), keepdims=True)
        out = (out - mu) * jax.lax.rsqrt(var + EPS)
        out = jnp.where(out >= 0, out, NEG_SLOPE * out)
        out = _refine(out, conv2_w, conv2_b, mask_w, mask_b, q_w, q_b, k_w, k_b, v_w, v_b)
        return residual + out

    def _gn(v, G=32, eps=1e-05):
        B_, C_, H_, W_ = v.shape
        g = v.reshape(B_, G, C_ // G, H_, W_)
        m = jnp.mean(g, axis=(2, 3, 4), keepdims=True)
        s = jnp.var(g, axis=(2, 3, 4), keepdims=True)
        return ((g - m) / jnp.sqrt(s + eps)).reshape(v.shape)

    def _ln_c(v, eps=1e-06):
        m = jnp.mean(v, axis=1, keepdims=True)
        s = jnp.var(v, axis=1, keepdims=True)
        return (v - m) / jnp.sqrt(s + eps)

    def _ln_t(v, eps=1e-05):
        m = jnp.mean(v, axis=-1, keepdims=True)
        s = jnp.var(v, axis=-1, keepdims=True)
        return (v - m) / jnp.sqrt(s + eps)

    def _to_tokens(v):
        B_, C_, H_, W_ = v.shape
        return v.reshape(B_, C_, H_ * W_).transpose(0, 2, 1)

    def _from_tokens(t, like):
        B_, C_, H_, W_ = like.shape
        return t.transpose(0, 2, 1).reshape(B_, C_, H_, W_)
    x = _L0_conv_ref(x, L0_conv_ln1_g, L0_conv_ln1_b, L0_conv_scale, L0_conv_q1, L0_conv_q3, L0_conv_k1, L0_conv_k3, L0_conv_v1, L0_conv_v3, L0_conv_o_w, L0_conv_ln2_g, L0_conv_ln2_b, L0_conv_g1, L0_conv_g3, L0_conv_i1, L0_conv_i3, L0_conv_r1)
    x = _L1_conv_ref(x, L1_conv_conv1_w, L1_conv_conv1_b, L1_conv_conv2_w, L1_conv_conv2_b, L1_conv_mask_w, L1_conv_mask_b, L1_conv_q_w, L1_conv_q_b, L1_conv_k_w, L1_conv_k_b, L1_conv_v_w, L1_conv_v_b)
    return x

_drawn_inputs = setup_inputs


def setup_inputs(seed=0):
    import zlib

    import numpy as np

    out = dict(_drawn_inputs(seed))
    spreads = {'L0_conv_ln1_g': (1.0, 0.6),
     'L0_conv_ln1_b': (0.0, 0.8),
     'L0_conv_ln2_g': (1.0, 0.6),
     'L0_conv_ln2_b': (0.0, 0.8)}
    factors = {'L0_conv_q1': 8.0,
     'L0_conv_q3': 8.0,
     'L0_conv_k1': 8.0,
     'L0_conv_k3': 8.0,
     'L0_conv_v1': 8.0,
     'L0_conv_v3': 8.0,
     'L0_conv_o_w': 8.0,
     'L0_conv_g1': 8.0,
     'L0_conv_g3': 8.0,
     'L0_conv_i1': 8.0,
     'L0_conv_i3': 8.0,
     'L0_conv_r1': 8.0,
     'L1_conv_conv1_b': 200.0,
     'L1_conv_conv2_b': 200.0,
     'L1_conv_q_w': 64.0,
     'L1_conv_q_b': 200.0,
     'L1_conv_k_w': 64.0,
     'L1_conv_k_b': 200.0,
     'L1_conv_v_b': 200.0,
     'L1_conv_conv1_w': 5.421,
     'L1_conv_conv2_w': 4.832,
     'L1_conv_mask_w': 8.0,
     'L1_conv_v_w': 8.0}
    for name, (base, spread) in spreads.items():
        noise = np.random.default_rng([zlib.crc32(name.encode()), seed]).standard_normal(out[name].shape)
        drawn = base * np.exp(spread * noise) if base else spread * noise
        out[name] = jnp.asarray(drawn.astype(out[name].dtype))
    for name, factor in factors.items():
        out[name] = (out[name] * factor).astype(out[name].dtype)
    return out
```

```python
from contextlib import ExitStack

import concourse.bass as bass
from concourse import mybir

F32 = mybir.dt.float32
BF16 = mybir.dt.bfloat16
ALU = mybir.AluOpType
ACT = mybir.ActivationFunctionType
AX = mybir.AxisListType

P = 128
B, C, H, W = 8, 32, 32, 32
PAIRS = B // 2
R = P // C
RH = H // R
BLK = RH * W
PW = W + 2
PLANE = (H + 2) * W
D = 4
EC = 64
EPS = 1e-5
SLOPE = 0.2
BANK = 512

TH, TW = 4, 8
KH, KW = TH + 2, TW + 2
KEYS = KH * KW
TA, TB = RH // TH, W // TW
UNITS = 2 * TA * TB
UPB = UNITS // 2
KSLOT = 64

K_EQ, K_HEAD, K_SELJ, K_AVG, K_ID, K_WIN = 0, 32, 160, 164, 292, 420
K_END = K_WIN + UPB * KEYS
V_BC1, V_BC2, V_BM, V_BQ, V_BK, V_BV, V_SCALE, V_LN, V_OW = 0, 1, 2, 3, 4, 5, 6, 7, 7 + 4 * W
V_END = V_OW + D * C


class Signal:

    def __init__(self, sem, per_pair, start):
        self.sem, self.per_pair, self.start = sem, per_pair, start

    def at(self, pair, k):
        assert k or self.start, self.sem
        return pair * self.per_pair + (k + self.start)

    def before(self, pair):
        return self.at(pair, 0)

    def done(self, pair):
        return self.at(pair, self.per_pair)


def build(nc, x, shape_consts, vectors, w1_qkv, w3_qkv, w1_gi, w3_gi, conv_w, l1_qkv, r1_t, out):
    with ExitStack() as ctx:
        def sb(name, shape, dt=F32):
            return ctx.enter_context(nc.sbuf_tensor(name, shape, dt))

        def sem(name):
            return ctx.enter_context(nc.semaphore(name))

        signals = []

        def signal(name, per_pair, start=0):
            signals.append(Signal(sem(name), per_pair, start))
            return signals[-1]

        ps = ctx.enter_context(nc.psum_tensor("ps", [P, 8, BANK], F32))

        kc = sb("kc", [P, K_END])
        vec = sb("vec", [P, V_END])
        w1a = sb("w1a", [C, 3 * C])
        w3a = sb("w3a", [C, 3, 3, 3 * C])
        w1b = sb("w1b", [EC, 2 * C])
        w3b = sb("w3b", [EC, 3, 2, 3 * EC])
        w_conv = sb("w_conv", [3 * C, 3, 3, C])
        w_qk = sb("w_qk", [3 * C, 3, 2 * C])
        w_v = sb("w_v", [3 * C, 3, C])
        w_gi = sb("w_gi", [3 * C, 2, 3, EC])
        w_bd = sb("w_bd", [P, 3, P])
        w_r1 = sb("w_r1", [P, 2, C])
        ident_bf = sb("ident_bf", [P, P], BF16)
        win_bf = sb("win_bf", [P, UPB * KEYS], BF16)
        inv_scale = sb("inv_scale", [P, 1])
        half_bm = sb("half_bm", [P, 1])
        zeros = sb("zeros", [P, 2, H + 2])
        ones = sb("ones", [P, 2 * BLK])
        neg_half = sb("neg_half", [P, 2 * RH])

        x_in = sb("x_in", [P, 2, BLK])
        x1 = sb("x1", [P, 2, BLK])
        x2_all = sb("x2_all", [P, B, BLK])
        out_all = sb("out_all", [P, B, BLK])

        ln1_out = sb("ln1_out", [P, 2, BLK])
        ln2_out = sb("ln2_out", [P, 2, BLK])
        act_in = sb("act_in", [P, 2, BLK])
        sh_ln1 = sb("sh_ln1", [3 * C, 2, PLANE])
        sh_ln2 = sb("sh_ln2", [3 * C, 2, PLANE])
        sh_x2 = sb("sh_x2", [3 * C, 2, PLANE])
        sh_in = sb("sh_in", [3 * C, 2, PLANE])
        ln_c = sb("ln_c", [P, 2 * RH, W])
        ln_q = sb("ln_q", [P, 2 * RH, W])
        ln_s = sb("ln_s", [P, 4, 2 * RH])
        qk_t = sb("qk_t", [P, 2, BANK])
        v4 = sb("v4", [P, 2, BLK])
        sc_m = sb("sc_m", [P, 2 * D, C])
        sc_d = sb("sc_d", [P, 2 * D])
        sm = sb("sm", [P, 4, 2 * D])
        mix_p = sb("mix_p", [P, 2, D, C])
        mix_s = sb("mix_s", [P, 2, C])
        mix = sb("mix", [P, 2, R, C])
        gate = sb("gate", [P, 2, BANK])
        gi = sb("gi", [P, 2, BANK])
        hn = sb("hn", [P, 2, BLK])
        hc = sb("hc", [P, 2, BLK])
        st6 = sb("st6", [P, 2, 6])
        st = sb("st", [P, 2, 2])
        sts = sb("sts", [P, 8, 2])
        th = sb("th", [P, 2 * BLK])
        msk = sb("msk", [P, 2 * BLK])
        omm = sb("omm", [P, 2 * BLK])
        xm = sb("xm", [P, 2, RH + 2, PW])
        q_bd = sb("q_bd", [P, UNITS, R, TH * TW])
        k_h = sb("k_h", [P, 2, RH + 2, PW])
        xw = sb("xw", [P, UNITS, KEYS])
        v_t = sb("v_t", [P, UNITS // 2, P])
        prob = sb("prob", [P, UNITS, KSLOT])
        wsm = sb("wsm", [P, 3, UNITS])
        p_t = sb("p_t", [P, UNITS // 2, P])
        out1 = sb("out1", [P, 2 * BLK])
        res = sb("res", [P, 2 * BLK])
        dif = sb("dif", [P, 2, RH, TB // 2, 2 * TW])

        s_consts, s_w, s_diag = sem("s_consts"), sem("s_w"), sem("s_diag")
        s_zero, s_zero_bd = sem("s_zero"), sem("s_zero_bd")
        s_fold, s_wready = sem("s_fold"), sem("s_wready")

        g_x = signal("x_loaded", 16 * R)
        g_ln = [signal("ln1_steps", 8), signal("ln2_steps", 8)]
        g_sq = [signal("ln1_squares", 1), signal("ln2_squares", 1)]
        g_rs = [signal("ln1_rstd", 1), signal("ln2_rstd", 1)]
        g_sh = [signal("ln1_shifted", 12 * 16, start=1), signal("ln2_shifted", 12 * 16, start=1)]
        g_qkt = signal("qkt_in_psum", 2)
        g_qkt_sb = signal("qkt_in_sbuf", 2)
        g_v4 = signal("v4_in_psum", 1, start=1)
        g_v4_sb = signal("v4_in_sbuf", 1)
        g_gram = signal("gram_in_psum", 1, start=1)
        g_score = signal("score_steps", 11)
        g_rep = signal("scores_by_head", 1)
        g_pexp = signal("head_exp", 1)
        g_y = signal("attn_out_in_psum", 1, start=1)
        g_x1 = signal("x1_done", 1)
        g_g = signal("gate_in_psum", 2)
        g_i = signal("info_in_psum", 2, start=1)
        g_gelu = signal("gelu_done", 2)
        g_gi = signal("gated", 2, start=1)
        g_r1 = signal("r1_in_psum", 1, start=1)
        g_x2 = signal("x2_done", 1, start=1)
        g_fix = [signal(f"edges_zeroed_{n}", 2) for n in ("ln1", "ln2", "x2", "in")]
        g_xw = signal("key_windows", 2 * TA)
        g_x2sh = signal("x2_shifted", 12 * 16)
        g_c1 = signal("conv1_in_psum", 1, start=1)
        g_c1_sb = signal("conv1_in_sbuf", 1)
        g_in = signal("inorm_steps", 8)
        g_avg = signal("inorm_averages", 2, start=1)
        g_inr = signal("inorm_rstd", 1)
        g_act = signal("inorm_applied", 2, start=1)
        g_lr = signal("lrelu_done", 1, start=1)
        g_insh = signal("in_shifted", 12 * 16, start=1)
        g_mk = signal("mask_in_psum", 1)
        g_c2 = signal("conv2_in_psum", 1, start=1)
        g_th = signal("tanh_done", 1)
        g_xm = signal("masked_steps", 2, start=1)
        g_halo = signal("halo_loaded", 2 * 16, start=1)
        g_q = signal("q_in_psum", 1)
        g_k = signal("k_in_psum", 1)
        g_v = signal("v_in_psum", 1, start=1)
        g_q_sb = signal("q_in_sbuf", 4)
        g_k_sb = signal("k_in_sbuf", 2)
        g_v_sb = signal("v_in_sbuf", 2)
        g_s = signal("sims_in_psum", 1, start=1)
        g_sm = signal("window_softmax_steps", 5)
        g_we = signal("window_exp", 1)
        g_t = signal("probs_t_in_psum", 2, start=1)
        g_t_sb = signal("probs_t_in_sbuf", 2, start=1)
        g_pv = signal("window_out_in_psum", 1, start=1)
        g_o1 = signal("out1_in_sbuf", 1)
        g_res = signal("residual_steps", 2, start=1)
        g_fin = signal("final_steps", 4, start=1)
        g_out = signal("out_stored", 16 * R)

        block = ctx.enter_context(nc.Block())

        x_dram = x.rearrange("b c (r q) w -> r c b (q w)", r=R)
        out_dram = out.rearrange("b c (r q) w -> r c b (q w)", r=R)

        def images(t, pair):
            return t[:, bass.ts(pair, 2)]

        def alone(engine):
            engine.wait_ge(s_zero, Z_PADS)

        def flat(t):
            return t.rearrange("p i m -> p (i m)")

        def plane(t):
            return t[:, :, :].rearrange("p i (y x) -> p i y x", x=W)

        Z_PADS = 8

        @block.sync
        def _(sp):
            def load_x(pair):
                for r in range(R):
                    sp.dma_start(x_in[C * r:C * r + C, :, :],
                                 x_dram[r][:, bass.ts(pair, 2), :]).then_inc(g_x.sem, 16)

            def spread(src, planes, done):
                for r in range(R):
                    for s in range(3):
                        start = (1 + RH * r) * W + 1 - s
                        sp.dma_start(planes[C * s:C * s + C, :, start:start + BLK], src[C * r:C * r + C])\
                          .then_inc(done.sem, 16)

            load_x(0)
            sp.dma_start(vec[:, :], vectors).then_inc(s_consts, 16)
            sp.dma_start(w1a[:, :], w1_qkv).then_inc(s_w, 16)
            sp.dma_start(w3a[:, :, :, :], w3_qkv).then_inc(s_w, 16)
            sp.dma_start(w1b[:, :], w1_gi).then_inc(s_w, 16)
            sp.dma_start(w3b[:, :, :, :], w3_gi).then_inc(s_w, 16)
            for g in signals:
                if g.start:
                    sp.sem_inc(g.sem, g.start)
            sp.wait_ge(s_zero, Z_PADS)

            def front_1(pair):
                sp.wait_ge(g_v4.sem, g_v4.before(pair))
                sp.wait_ge(g_ln[0].sem, g_ln[0].done(pair))
                spread(ln1_out, sh_ln1, g_sh[0])

            def front_2(pair):
                sp.wait_ge(g_ln[1].sem, g_ln[1].done(pair))
                sp.wait_ge(g_i.sem, g_i.before(pair))
                spread(ln2_out, sh_ln2, g_sh[1])

            def back_1(pair):
                sp.wait_ge(g_x2.sem, g_x2.done(pair))
                alone(sp)
                sp.wait_ge(g_c1.sem, g_c1.before(pair))
                spread(images(x2_all, pair), sh_x2, g_x2sh)

            def back_2(pair):
                sp.wait_ge(g_lr.sem, g_lr.done(pair))
                sp.wait_ge(g_c2.sem, g_c2.before(pair))
                spread(act_in, sh_in, g_insh)

            def back_3(pair):
                sp.wait_ge(g_xm.sem, g_xm.at(pair, 2))
                sp.dma_start(xm[C:P, :, 0, :], xm[0:P - C, :, RH, :]).then_inc(g_halo.sem, 16)
                sp.dma_start(xm[0:P - C, :, RH + 1, :], xm[C:P, :, 1, :]).then_inc(g_halo.sem, 16)

            def back_4(pair):
                alone(sp)
                sp.wait_ge(g_fin.sem, g_fin.done(pair))
                for r in range(R):
                    sp.dma_start(out_dram[r][:, bass.ts(pair, 2), :],
                                 out_all[C * r:C * r + C, bass.ts(pair, 2), :]).then_inc(g_out.sem, 16)

            def load_next(pair):
                alone(sp)
                sp.wait_ge(g_x1.sem, g_x1.done(pair))
                load_x(pair + 1)

            with sp.Fori(0, PAIRS - 1) as pair:
                front_1(pair)
                load_next(pair)
                front_2(pair)
                back_1(pair)
                back_2(pair)
                back_3(pair)
                back_4(pair)
            last = PAIRS - 1
            front_1(last)
            front_2(last)
            back_1(last)
            back_2(last)
            back_3(last)
            back_4(last)
            sp.wait_ge(g_out.sem, g_out.done(last))

        @block.gpsimd
        def _(pool):
            for t in (sh_ln1, sh_ln2, sh_x2, sh_in, xm):
                nc.gpsimd.memset(t[:], 0.0).then_inc(s_zero, 1)
            nc.gpsimd.memset(neg_half[:, :], -0.5).then_inc(s_zero, 1)
            nc.gpsimd.memset(zeros[:, :, :], 0.0).then_inc(s_zero, 1)
            nc.gpsimd.memset(ones[:, :], 1.0).then_inc(s_zero, 1)
            pool.wait_ge(s_zero, Z_PADS)

            def rstd(g, rs, pair):
                pool.wait_ge(g.sem, g.at(pair, 5))
                nc.gpsimd.tensor_tensor(ln_s[:, 3, :], ln_s[:, 2, :], neg_half[:, :], ALU.pow)\
                  .then_inc(rs.sem, 1)

            def zero_edges(n, loaded, planes, pair):
                pool.wait_ge(loaded.sem, loaded.done(pair))
                for s, col in ((0, 0), (2, W - 1)):
                    at = slice(C * s, C * s + C)
                    nc.gpsimd.tensor_tensor(plane(planes)[at, :, :, col], zeros[at, :, :], zeros[at, :, :],
                                            ALU.add).then_inc(g_fix[n].sem, 1)

            def inorm_rstd(pair):
                pool.wait_ge(g_in.sem, g_in.at(pair, 6))
                nc.gpsimd.tensor_tensor(sts[:, 6, :], sts[:, 4, :], neg_half[:, 0:2], ALU.pow)\
                  .then_inc(g_inr.sem, 1)

            def residual(pair):
                pool.wait_ge(g_xm.sem, g_xm.at(pair, 1))
                pool.wait_ge(g_fin.sem, g_fin.before(pair))
                nc.gpsimd.tensor_tensor(omm[:, :], ones[:, :], msk[:, :], ALU.subtract)\
                  .then_inc(g_res.sem, 1)
                pool.wait_ge(g_o1.sem, g_o1.done(pair))
                pool.wait_ge(g_x2.sem, g_x2.done(pair))
                nc.gpsimd.tensor_tensor(res[:, :], out1[:, :], flat(images(x2_all, pair)), ALU.add)\
                  .then_inc(g_res.sem, 1)

            def one(pair):
                rstd(g_ln[0], g_rs[0], pair)
                zero_edges(0, g_sh[0], sh_ln1, pair)
                rstd(g_ln[1], g_rs[1], pair)
                zero_edges(1, g_sh[1], sh_ln2, pair)
                zero_edges(2, g_x2sh, sh_x2, pair)
                inorm_rstd(pair)
                zero_edges(3, g_insh, sh_in, pair)
                residual(pair)

            with pool.Fori(0, PAIRS) as pair:
                one(pair)

        @block.scalar
        def _(act):
            act.dma_start(kc[:, :], shape_consts).then_inc(s_consts, 16)
            act.dma_start(w_conv[:, :, :, :], conv_w).then_inc(s_diag, 16)
            act.wait_ge(s_zero_bd, 2)
            for r in range(R):
                act.dma_start(w_bd[C * r:C * r + C, :, C * r:C * r + C], l1_qkv).then_inc(s_diag, 16)
            for h in range(2):
                act.dma_start(w_r1[EC * h:EC * h + EC, h, :], r1_t).then_inc(s_diag, 16)

            def squares(g, sq, pair):
                act.wait_ge(g.sem, g.at(pair, 3))
                nc.scalar.activation(ln_q[:, :, :], ln_c[:, :, :], ACT.Square).then_inc(sq.sem, 1)

            def front_qkv(pair):
                for i in range(2):
                    act.wait_ge(g_qkt.sem, g_qkt.at(pair, i + 1))
                    act.wait_ge(g_gram.sem, g_gram.before(pair))
                    nc.scalar.activation(qk_t[:, i, :], ps[:, i, :], ACT.Copy).then_inc(g_qkt_sb.sem, 1)
                act.wait_ge(g_v4.sem, g_v4.done(pair))
                act.wait_ge(g_y.sem, g_y.before(pair))
                nc.scalar.activation(v4[:, :, :].rearrange("p i m -> p (i m)"), ps[:, 2, :], ACT.Copy)\
                  .then_inc(g_v4_sb.sem, 1)

            def head_exp(pair):
                act.wait_ge(g_score.sem, g_score.at(pair, 5))
                nc.scalar.activation(sm[:, 2, :], sm[:, 1, :], ACT.Exp).then_inc(g_pexp.sem, 1)

            def gelu(pair):
                for i in range(2):
                    act.wait_ge(g_g.sem, g_g.at(pair, i + 1))
                    act.wait_ge(g_gi.sem, g_gi.before(pair))
                    nc.scalar.activation(gate[:, i, :], ps[:, (1, 3)[i], :], ACT.Gelu).then_inc(g_gelu.sem, 1)

            def conv1_evac(pair):
                act.wait_ge(g_c1.sem, g_c1.done(pair))
                act.wait_ge(g_act.sem, g_act.before(pair))
                nc.scalar.activation(hc[:, :, :].rearrange("p i m -> p (i m)"), ps[:, 4, :], ACT.Identity,
                                     bias=vec[:, V_BC1:V_BC1 + 1]).then_inc(g_c1_sb.sem, 1)

            def inorm_apply(pair):
                act.wait_ge(g_in.sem, g_in.done(pair))
                act.wait_ge(g_lr.sem, g_lr.before(pair))
                for i in range(2):
                    nc.scalar.activation(hn[:, i, :], hc[:, i, :], ACT.Identity,
                                         bias=sts[:, 7, i:i + 1], scale=sts[:, 6, i:i + 1])\
                      .then_inc(g_act.sem, 1)

            def tanh_mask(pair):
                act.wait_ge(g_mk.sem, g_mk.done(pair))
                act.wait_ge(g_xm.sem, g_xm.before(pair))
                act.wait_ge(g_res.sem, g_res.before(pair))
                nc.scalar.activation(th[:, :], ps[:, 6, :], ACT.Tanh, bias=half_bm[:, 0:1], scale=0.5)\
                  .then_inc(g_th.sem, 1)

            def out1_evac(pair):
                act.wait_ge(g_c2.sem, g_c2.done(pair))
                act.wait_ge(g_fin.sem, g_fin.before(pair))
                act.wait_ge(g_res.sem, g_res.before(pair))
                nc.scalar.activation(out1[:, :], ps[:, 7, :], ACT.Identity, bias=vec[:, V_BC2:V_BC2 + 1])\
                  .then_inc(g_o1.sem, 1)

            def qk_evac(pair):
                act.wait_ge(g_q.sem, g_q.done(pair))
                act.wait_ge(g_s.sem, g_s.before(pair))
                for r in range(R):
                    rows = slice(C * r, C * r + C)
                    nc.scalar.activation(q_bd[rows, :, r, :],
                                         ps[rows, 4, :].rearrange("p (u m) -> p u m", u=UNITS), ACT.Identity,
                                         bias=vec[rows, V_BQ:V_BQ + 1]).then_inc(g_q_sb.sem, 1)
                act.wait_ge(g_k.sem, g_k.done(pair))
                for i in range(2):
                    nc.scalar.activation(k_h[:, i, :, :].rearrange("p y x -> p (y x)"),
                                         ps[:, 5 + i, 0:(RH + 2) * PW], ACT.Identity,
                                         bias=vec[:, V_BK:V_BK + 1]).then_inc(g_k_sb.sem, 1)

            def key_windows(pair):
                act.wait_ge(g_halo.sem, g_halo.done(pair))
                act.wait_ge(g_v.sem, g_v.before(pair))
                for ia in range(2 * TA):
                    i, a = ia // TA, ia % TA
                    for b in range(TB):
                        ins = nc.scalar.activation(
                            xw[:, TB * ia + b, :].rearrange("p (y x) -> p y x", x=KW),
                            xm[:, i, TH * a:TH * a + KH, TW * b:TW * b + KW], ACT.Copy)
                    ins.then_inc(g_xw.sem, 1)

            def window_exp(pair):
                act.wait_ge(g_sm.sem, g_sm.at(pair, 2))
                nc.scalar.activation(prob[:, :, 0:KEYS], prob[:, :, 0:KEYS], ACT.Exp).then_inc(g_we.sem, 1)

            def probs_t(pair):
                act.wait_ge(g_pv.sem, g_pv.before(pair))
                for t in range(2):
                    act.wait_ge(g_t.sem, g_t.at(pair, t + 1))
                    nc.scalar.activation(p_t[:, 4 * t:4 * t + 4, :].rearrange("p u m -> p (u m)"),
                                         ps[:, (7, 4)[t], :], ACT.Copy).then_inc(g_t_sb.sem, 1)

            act.wait_ge(s_consts, 32)
            act.wait_ge(s_wready, 8)

            def one(pair):
                squares(g_ln[0], g_sq[0], pair)
                front_qkv(pair)
                head_exp(pair)
                squares(g_ln[1], g_sq[1], pair)
                gelu(pair)
                conv1_evac(pair)
                inorm_apply(pair)
                tanh_mask(pair)
                out1_evac(pair)
                qk_evac(pair)
                key_windows(pair)
                window_exp(pair)
                probs_t(pair)

            with act.Fori(0, PAIRS) as pair:
                one(pair)

        @block.vector
        def _(dve):
            for t in (w_bd, w_r1):
                nc.vector.memset(t[:], 0.0).then_inc(s_zero_bd, 1)
            for t in (q_bd, prob, ps):
                nc.vector.memset(t[:], 0.0).then_inc(s_zero_bd, 1)
            dve.wait_ge(s_consts, 32)
            nc.vector.tensor_copy(ident_bf[:, :], kc[:, K_ID:K_ID + P]).then_inc(s_wready, 1)
            nc.vector.tensor_copy(win_bf[:, :], kc[:, K_WIN:K_END]).then_inc(s_wready, 1)
            nc.vector.reciprocal(inv_scale[:, :], vec[:, V_SCALE:V_SCALE + 1]).then_inc(s_wready, 1)
            nc.vector.tensor_scalar(half_bm[:, :], vec[:, V_BM:V_BM + 1], 0.5, None, ALU.mult)\
              .then_inc(s_wready, 1)
            dve.wait_ge(s_fold, 2)
            qkv_f = ps[0:3 * C, 0, 0:9 * C].rearrange("p (m y o) -> p m y o", m=3, o=C)
            for m in range(2):
                nc.vector.tensor_copy(w_qk[:, :, C * m:C * m + C], qkv_f[:, m]).then_inc(s_wready, 1)
            nc.vector.tensor_copy(w_v[:, :, :], qkv_f[:, 2]).then_inc(s_wready, 1)
            nc.vector.tensor_copy(w_gi[:, :, :, :].rearrange("p m y o -> p (m y o)"),
                                  ps[0:3 * C, 1, 0:6 * EC]).then_inc(s_wready, 1)
            dve.wait_ge(s_wready, 8)
            dve.wait_ge(s_zero, Z_PADS)

            def layernorm(n, src, dst, pair, src_ready, dst_free):
                g, sq, rs = g_ln[n], g_sq[n], g_rs[n]
                x3 = src.rearrange("p i (y x) -> p (i y) x", x=W)
                rows = 2 * RH

                def per_row(k):
                    return ln_s[:, k, :].unsqueeze(2).broadcast_to([P, rows, W])

                def per_col(k):
                    return vec[:, V_LN + W * k:V_LN + W * k + W].unsqueeze(1).broadcast_to([P, rows, W])

                src_ready()
                nc.vector.reduce_sum(ln_s[:, 0, :], x3, AX.X).then_inc(g.sem, 1)
                dve.wait_ge(g.sem, g.at(pair, 1))
                nc.vector.tensor_scalar(ln_s[:, 0, :], ln_s[:, 0, :], 1.0 / W, None, ALU.mult)\
                  .then_inc(g.sem, 1)
                dve.wait_ge(g.sem, g.at(pair, 2))
                nc.vector.tensor_tensor(ln_c[:, :, :], x3, per_row(0), ALU.subtract).then_inc(g.sem, 1)
                dve.wait_ge(sq.sem, sq.done(pair))
                nc.vector.reduce_sum(ln_s[:, 1, :], ln_q[:, :, :], AX.X).then_inc(g.sem, 1)
                dve.wait_ge(g.sem, g.at(pair, 4))
                nc.vector.tensor_scalar(ln_s[:, 2, :], ln_s[:, 1, :], 1.0 / W, EPS, ALU.mult, ALU.add)\
                  .then_inc(g.sem, 1)
                dve.wait_ge(rs.sem, rs.done(pair))
                nc.vector.tensor_tensor(ln_c[:, :, :], ln_c[:, :, :], per_row(3), ALU.mult).then_inc(g.sem, 1)
                dve.wait_ge(g.sem, g.at(pair, 6))
                nc.vector.tensor_tensor(ln_c[:, :, :], ln_c[:, :, :], per_col(2 * n), ALU.mult)\
                  .then_inc(g.sem, 1)
                dve.wait_ge(g.sem, g.at(pair, 7))
                dst_free()
                nc.vector.tensor_tensor(dst[:, :, :].rearrange("p i (y x) -> p (i y) x", x=W),
                                        ln_c[:, :, :], per_col(2 * n + 1), ALU.add).then_inc(g.sem, 1)

            def ln1(pair):
                layernorm(0, x_in[:, :, :], ln1_out, pair,
                          lambda: dve.wait_ge(g_x.sem, g_x.done(pair)),
                          lambda: dve.wait_ge(g_sh[0].sem, g_sh[0].before(pair)))

            def scores(pair):
                g = g_score
                dve.wait_ge(g_gram.sem, g_gram.done(pair))
                eq = kc[:, K_EQ:K_EQ + C].unsqueeze(1).broadcast_to([P, 2 * D, C])
                nc.vector.tensor_tensor(sc_m[:, :, :], ps[:, 3, 0:2 * P].rearrange("p (e c) -> p e c", c=C),
                                        eq, ALU.mult).then_inc(g.sem, 1)
                dve.wait_ge(g.sem, g.at(pair, 1))
                nc.vector.reduce_sum(sc_d[:, :], sc_m[:, :, :], AX.X).then_inc(g.sem, 1)
                dve.wait_ge(g_rep.sem, g_rep.done(pair))
                nc.vector.tensor_scalar(sm[:, 0, :], ps[:, 3, 2 * P:2 * P + 2 * D], inv_scale[:, 0:1], None,
                                        ALU.mult).then_inc(g.sem, 1)
                dve.wait_ge(g.sem, g.at(pair, 3))
                sm3 = [sm[:, k, :].rearrange("p (i e) -> p i e", e=D) for k in range(3)]

                def per_image(col):
                    return sm[:, 3, col:col + 2].unsqueeze(2).broadcast_to([P, 2, D])

                nc.vector.reduce_max(sm[:, 3, 0:2], sm3[0], AX.X).then_inc(g.sem, 1)
                dve.wait_ge(g.sem, g.at(pair, 4))
                nc.vector.tensor_tensor(sm3[1], sm3[0], per_image(0), ALU.subtract).then_inc(g.sem, 1)
                dve.wait_ge(g_pexp.sem, g_pexp.done(pair))
                nc.vector.reduce_sum(sm[:, 3, 2:4], sm3[2], AX.X).then_inc(g.sem, 1)
                dve.wait_ge(g.sem, g.at(pair, 6))
                nc.vector.reciprocal(sm[:, 3, 4:6], sm[:, 3, 2:4]).then_inc(g.sem, 1)
                dve.wait_ge(g.sem, g.at(pair, 7))
                nc.vector.tensor_tensor(sm3[0], sm3[2], per_image(4), ALU.mult).then_inc(g.sem, 1)
                dve.wait_ge(g.sem, g.at(pair, 8))
                for i in range(2):
                    p_b = sm[:, 0, D * i:D * i + D].unsqueeze(2).broadcast_to([P, D, C])
                    ow = vec[:, V_OW:V_OW + D * C].rearrange("p (e o) -> p e o", o=C)
                    mul = nc.vector.tensor_tensor(mix_p[:, i, :, :], ow, p_b, ALU.mult)
                mul.then_inc(g.sem, 1)
                dve.wait_ge(g.sem, g.at(pair, 9))
                nc.vector.reduce_sum(mix_s[:, :, :], mix_p[:, :, :, :].rearrange("p i e o -> p i o e"), AX.X)\
                  .then_inc(g.sem, 1)
                dve.wait_ge(g.sem, g.at(pair, 10))
                sel = kc[:, K_SELJ:K_SELJ + R].unsqueeze(2).broadcast_to([P, R, C])
                for i in range(2):
                    mul = nc.vector.tensor_tensor(mix[:, i, :, :], sel,
                                                  mix_s[:, i, :].unsqueeze(1).broadcast_to([P, R, C]), ALU.mult)
                mul.then_inc(g.sem, 1)

            def ln2(pair):
                def x1_sum():
                    dve.wait_ge(g_y.sem, g_y.done(pair))
                    nc.vector.tensor_tensor(flat(x1[:, :, :]), ps[:, 0, :], flat(x_in[:, :, :]), ALU.add)\
                      .then_inc(g_x1.sem, 1)
                    dve.wait_ge(g_x1.sem, g_x1.done(pair))
                layernorm(1, x1[:, :, :], ln2_out, pair, x1_sum,
                          lambda: dve.wait_ge(g_sh[1].sem, g_sh[1].before(pair)))

            def gated(pair):
                for i in range(2):
                    dve.wait_ge(g_gelu.sem, g_gelu.at(pair, i + 1))
                    dve.wait_ge(g_i.sem, g_i.at(pair, i + 1))
                    dve.wait_ge(g_r1.sem, g_r1.before(pair))
                    nc.vector.tensor_tensor(gi[:, i, :], ps[:, (2, 0)[i], :], gate[:, i, :], ALU.mult)\
                      .then_inc(g_gi.sem, 1)

            def x2_sum(pair):
                dve.wait_ge(g_r1.sem, g_r1.done(pair))
                nc.vector.tensor_tensor(flat(images(x2_all, pair)), ps[:, 1, :], flat(x1[:, :, :]),
                                        ALU.add)\
                  .then_inc(g_x2.sem, 1)

            def inorm(pair):
                g = g_in
                dve.wait_ge(g_c1_sb.sem, g_c1_sb.done(pair))
                dve.wait_ge(g_avg.sem, g_avg.before(pair))
                for i in range(2):
                    ins = nc.vector.bn_stats(st6[:, i, :], hc[:, i, :])
                ins.then_inc(g.sem, 1)
                dve.wait_ge(g.sem, g.at(pair, 1))
                nc.vector.memset(sts[:, 3, :], 0.0)
                for i in range(2):
                    ins = nc.vector.bn_aggr(st[:, i, :], st6[:, i, :])
                ins.then_inc(g.sem, 1)
                dve.wait_ge(g_avg.sem, g_avg.at(pair, 1))
                nc.vector.tensor_copy(sts[:, 0, :], ps[:, 5, 0:2]).then_inc(g.sem, 1)
                dve.wait_ge(g.sem, g.at(pair, 3))
                nc.vector.tensor_tensor(sts[:, 1, :], st[:, :, 0], sts[:, 0, :], ALU.subtract).then_inc(g.sem, 1)
                dve.wait_ge(g.sem, g.at(pair, 4))
                for i in range(2):
                    ins = nc.vector.scalar_tensor_tensor(
                        out=sts[:, 2, i:i + 1], in0=sts[:, 1, i:i + 1], scalar=sts[:, 1, i:i + 1],
                        in1=st[:, i, 1:2], op0=ALU.mult, op1=ALU.add)
                ins.then_inc(g.sem, 1)
                dve.wait_ge(g_avg.sem, g_avg.at(pair, 2))
                nc.vector.tensor_scalar(sts[:, 4, :], ps[:, 5, 2:4], EPS, None, ALU.add).then_inc(g.sem, 1)
                dve.wait_ge(g_inr.sem, g_inr.done(pair))
                for i in range(2):
                    ins = nc.vector.scalar_tensor_tensor(
                        out=sts[:, 7, i:i + 1], in0=sts[:, 0, i:i + 1], scalar=-1.0,
                        in1=sts[:, 6, i:i + 1], op0=ALU.mult, op1=ALU.mult)
                ins.then_inc(g.sem, 2)

            def lrelu(pair):
                dve.wait_ge(g_act.sem, g_act.done(pair))
                dve.wait_ge(g_insh.sem, g_insh.before(pair))
                dve.wait_ge(g_xm.sem, g_xm.before(pair))
                nc.vector.scalar_tensor_tensor(out=flat(act_in[:, :, :]), in0=flat(hn[:, :, :]), scalar=SLOPE,
                                               in1=flat(hn[:, :, :]), op0=ALU.mult, op1=ALU.max)\
                  .then_inc(g_lr.sem, 1)

            def masked(pair):
                dve.wait_ge(g_th.sem, g_th.done(pair))
                nc.vector.tensor_scalar(msk[:, :], th[:, :], 0.5, 0.5, ALU.mult, ALU.add).then_inc(g_xm.sem, 1)
                dve.wait_ge(g_xm.sem, g_xm.at(pair, 1))
                dve.wait_ge(g_v.sem, g_v.before(pair))
                dve.wait_ge(g_halo.sem, g_halo.before(pair))
                nc.vector.tensor_tensor(xm[:, :, 1:1 + RH, 1:1 + W],
                                        msk[:, :].rearrange("p (i y x) -> p i y x", i=2, x=W),
                                        act_in[:, :, :].rearrange("p i (y x) -> p i y x", x=W), ALU.mult).then_inc(g_xm.sem, 1)

            def v_evac(pair):
                dve.wait_ge(g_v.sem, g_v.done(pair))
                dve.wait_ge(g_pv.sem, g_pv.before(pair))
                for h in range(2):
                    nc.vector.tensor_copy(v_t[:, 4 * h:4 * h + 4, :].rearrange("p u m -> p (u m)"),
                                          ps[:, (7, 4)[h], :]).then_inc(g_v_sb.sem, 1)

            def window_softmax(pair):
                g = g_sm
                sims = ps[:, 5:7, 0:UPB * KEYS].rearrange("p b (u k) -> p b u k", k=KEYS)
                pr4 = prob[:, :, 0:KEYS].rearrange("p (b u) k -> p b u k", b=2)

                def per_tile(k):
                    return wsm[:, k, :].unsqueeze(2).broadcast_to([P, UNITS, KEYS])

                dve.wait_ge(g_s.sem, g_s.done(pair))
                dve.wait_ge(g_t.sem, g_t.before(pair))
                nc.vector.reduce_max(wsm[:, 0, :].rearrange("p (b u) -> p b u", b=2), sims, AX.X)\
                  .then_inc(g.sem, 1)
                dve.wait_ge(g.sem, g.at(pair, 1))
                nc.vector.tensor_tensor(pr4, sims, wsm[:, 0, :].rearrange("p (b u) -> p b u", b=2)
                                        .unsqueeze(3).broadcast_to([P, 2, UPB, KEYS]), ALU.subtract)\
                  .then_inc(g.sem, 1)
                dve.wait_ge(g_we.sem, g_we.done(pair))
                nc.vector.reduce_sum(wsm[:, 1, :], prob[:, :, 0:KEYS], AX.X).then_inc(g.sem, 1)
                dve.wait_ge(g.sem, g.at(pair, 3))
                nc.vector.reciprocal(wsm[:, 2, :], wsm[:, 1, :]).then_inc(g.sem, 1)
                dve.wait_ge(g.sem, g.at(pair, 4))
                nc.vector.tensor_tensor(prob[:, :, 0:KEYS], prob[:, :, 0:KEYS], per_tile(2), ALU.mult)\
                  .then_inc(g.sem, 1)

            def final(pair):
                g = g_fin
                dve.wait_ge(g_pv.sem, g_pv.done(pair))
                dve.wait_ge(g_o1.sem, g_o1.done(pair))
                o1 = out1[:, :].rearrange("p (q b h x) -> p q b h x", b=TB // 2, h=2, x=TW)
                dv = dif[:, :, :, :, :].rearrange("p i y b (h x) -> p (i y) b h x", h=2)
                for h in range(2):
                    att = ps[:, 5 + h, :].rearrange("p (q b h x) -> p q b h x", b=TB // 2, h=2, x=TW)
                    nc.vector.scalar_tensor_tensor(
                        out=dv[:, :, :, h, :].rearrange("p q b x -> p (q b) x"),
                        in0=att[:, :, :, h, :].rearrange("p q b x -> p (q b) x"),
                        scalar=vec[:, V_BV:V_BV + 1],
                        in1=o1[:, :, :, h, :].rearrange("p q b x -> p (q b) x"),
                        op0=ALU.add, op1=ALU.subtract).then_inc(g.sem, 1)
                dve.wait_ge(g.sem, g.at(pair, 2))
                dve.wait_ge(g_res.sem, g_res.done(pair))
                d2 = dif[:].rearrange("p i y b x -> p (i y b x)")
                nc.vector.tensor_tensor(d2, d2, omm[:, :], ALU.mult).then_inc(g.sem, 1)
                dve.wait_ge(g.sem, g.at(pair, 3))
                nc.vector.tensor_tensor(images(out_all, pair).rearrange("p i m -> p (i m)"), d2, res[:, :],
                                        ALU.add).then_inc(g.sem, 1)

            def one(pair):
                ln1(pair)
                scores(pair)
                ln2(pair)
                gated(pair)
                x2_sum(pair)
                inorm(pair)
                lrelu(pair)
                masked(pair)
                v_evac(pair)
                window_softmax(pair)
                final(pair)

            with dve.Fori(0, PAIRS) as pair:
                one(pair)

        @block.tensor
        def _(pe):
            pe.wait_ge(s_w, 64)
            pe.wait_ge(s_zero_bd, 5)
            for m in range(3):
                for s in range(3):
                    mm = nc.tensor.matmul(ps[C * s:C * s + C, 0, 3 * C * m:3 * C * m + 3 * C],
                                          w1a[:, C * m:C * m + C], w3a[:, s, m, :], start=True, stop=True)
            mm.then_inc(s_fold, 1)
            for m in range(2):
                for s in range(3):
                    mm = nc.tensor.matmul(ps[C * s:C * s + C, 1, 3 * EC * m:3 * EC * m + 3 * EC],
                                          w1b[:, C * m:C * m + C], w3b[:, s, m, :], start=True, stop=True)
            mm.then_inc(s_fold, 1)
            pe.wait_ge(s_wready, 8)
            pe.wait_ge(s_diag, 16 * (1 + R + 2))
            pe.wait_ge(s_consts, 32)

            def block_conv(planes, bank, weight):
                for dy in range(3):
                    for r in range(R):
                        mm = nc.tensor.matmul(ps[C * r:C * r + C, bank, :], weight(dy),
                                              plane(planes)[:, :, RH * r + dy:RH * r + dy + RH, 0:W],
                                              start=(dy == 0), stop=(dy == 2))
                return mm

            def qkv(pair):
                xs = plane(sh_ln1)
                pe.wait_ge(g_fix[0].sem, g_fix[0].done(pair))
                pe.wait_ge(g_x2.sem, g_x2.before(pair))
                for i in range(2):
                    for h in range(2):
                        for d in range(D):
                            to = ps[:, i, P * 2 * h:P * 2 * h + 2 * P]\
                                .rearrange("p (m d c) -> p m d c", m=2, d=D)[:, :, d, :]
                            for dy in range(3):
                                y = H // 2 * h + dy
                                mm = nc.tensor.matmul(to, sh_ln1[:, i, W * y + d:W * y + d + D * P - D + 1:D],
                                                      w_qk[:, dy, :], start=(dy == 0), stop=(dy == 2))
                    mm.then_inc(g_qkt.sem, 1)
                for dy in range(3):
                    for d in range(D):
                        mm = nc.tensor.matmul(ps[C * d:C * d + C, 2, :], w_v[:, dy, :],
                                              xs[:, :, dy:dy + H, d:d + W - D + 1:D],
                                              start=(dy == 0), stop=(dy == 2))
                mm.then_inc(g_v4.sem, 1)

            def gram(pair):
                for i in range(2):
                    pe.wait_ge(g_qkt_sb.sem, g_qkt_sb.at(pair, i + 1))
                    t = qk_t[:, i, :].rearrange("p (h m k) -> p h m k", h=2, m=2)
                    for h in range(2):
                        mm = nc.tensor.matmul(ps[:, 3, P * i:P * i + P], t[:, h, 1, :], t[:, h, 0, :],
                                              start=(h == 0), stop=(h == 1))
                mm.then_inc(g_gram.sem, 1)

            def by_head(pair):
                pe.wait_ge(g_score.sem, g_score.at(pair, 2))
                nc.tensor.matmul(ps[:, 3, 2 * P:2 * P + 2 * D], kc[:, K_HEAD:K_HEAD + P], sc_d[:, :],
                                 start=True, stop=True).then_inc(g_rep.sem, 1)

            def attn_out(pair):
                pe.wait_ge(g_score.sem, g_score.done(pair))
                pe.wait_ge(g_v4_sb.sem, g_v4_sb.done(pair))
                for i in range(2):
                    mm = nc.tensor.matmul(ps[:, 0, BLK * i:BLK * i + BLK],
                                          mix[:, i, :, :].rearrange("p j o -> p (j o)"), v4[:, i, :],
                                          start=True, stop=True)
                mm.then_inc(g_y.sem, 1)

            def gate_info(pair):
                xs = plane(sh_ln2)
                pe.wait_ge(g_fix[1].sem, g_fix[1].done(pair))
                for i in range(2):
                    for m, bank, g in ((0, (1, 3)[i], g_g), (1, (2, 0)[i], g_i)):
                        for dy in range(3):
                            for h in range(2):
                                y = H // 2 * h + dy
                                mm = nc.tensor.matmul(ps[EC * h:EC * h + EC, bank, :], w_gi[:, m, dy, :],
                                                      xs[:, i, y:y + H // 2, 0:W],
                                                      start=(dy == 0), stop=(dy == 2))
                        mm.then_inc(g.sem, 1)

            def reduce_1(pair):
                pe.wait_ge(g_gi.sem, g_gi.done(pair))
                for r in range(R):
                    mm = nc.tensor.matmul(ps[C * r:C * r + C, 1, :], w_r1[:, r // 2, :],
                                          gi[:, :, BLK * (r % 2):BLK * (r % 2) + BLK], start=True, stop=True)
                mm.then_inc(g_r1.sem, 1)

            def conv1(pair):
                pe.wait_ge(g_fix[2].sem, g_fix[2].done(pair))
                pe.wait_ge(g_t_sb.sem, g_t_sb.before(pair))
                block_conv(sh_x2, 4, lambda dy: w_conv[:, 0, dy, :]).then_inc(g_c1.sem, 1)

            def averages(pair):
                avg = kc[:, K_AVG:K_AVG + P]
                pe.wait_ge(g_in.sem, g_in.at(pair, 2))
                pe.wait_ge(g_fin.sem, g_fin.before(pair))
                nc.tensor.matmul(ps[:, 5, 0:2], avg, st[:, :, 0], start=True, stop=True).then_inc(g_avg.sem, 1)
                pe.wait_ge(g_in.sem, g_in.at(pair, 5))
                nc.tensor.matmul(ps[:, 5, 2:4], avg, sts[:, 2, :], start=True, stop=True).then_inc(g_avg.sem, 1)

            def conv2(pair):
                pe.wait_ge(g_fix[3].sem, g_fix[3].done(pair))
                block_conv(sh_in, 6, lambda dy: w_conv[:, 2, dy, :]).then_inc(g_mk.sem, 1)
                block_conv(sh_in, 7, lambda dy: w_conv[:, 1, dy, :]).then_inc(g_c2.sem, 1)

            def window_qkv(pair):
                pe.wait_ge(g_xm.sem, g_xm.done(pair))
                for ia in range(2 * TA):
                    i, a = ia // TA, ia % TA
                    rhs = xm[:, i, 1 + TH * a:1 + TH * a + TH, 1:1 + W]\
                        .rearrange("p y (b x) -> p b y x", x=TW)
                    mm = nc.tensor.matmul(ps[:, 4, P * ia:P * ia + P], w_bd[:, 0, :], rhs, start=True, stop=True)
                mm.then_inc(g_q.sem, 1)
                pe.wait_ge(g_halo.sem, g_halo.done(pair))
                pe.wait_ge(g_in.sem, g_in.at(pair, 6))
                pe.wait_ge(g_th.sem, g_th.done(pair))
                for i in range(2):
                    mm = nc.tensor.matmul(ps[:, 5 + i, 0:(RH + 2) * PW], w_bd[:, 1, :],
                                          xm[:, i, :, :].rearrange("p y x -> p (y x)"), start=True, stop=True)
                mm.then_inc(g_k.sem, 1)
                pe.wait_ge(g_o1.sem, g_o1.done(pair))
                pe.wait_ge(g_q_sb.sem, g_q_sb.done(pair))
                pe.wait_ge(g_xw.sem, g_xw.done(pair))
                for u in range(UNITS):
                    half, t = u % 2, u // 2
                    mm = nc.tensor.matmul(ps[KSLOT * half:KSLOT * half + KEYS, (7, 4)[t // 4],
                                             P * (t % 4):P * (t % 4) + P],
                                          xw[:, u, :], w_bd[:, 2, :], start=True, stop=True)
                mm.then_inc(g_v.sem, 1)

            def window_scores(pair):
                pe.wait_ge(g_k_sb.sem, g_k_sb.done(pair))
                for bank in range(2):
                    nc.tensor.matmul(ps[:, 5 + bank, 0:UPB * KEYS], ident_bf[:, :], win_bf[:, :],
                                     start=True, stop=False, skip_group_check=True)
                    for n in range(UPB):
                        u = UPB * bank + n
                        i, a, b = u // (TA * TB), u // TB % TA, u % TB
                        mm = nc.tensor.matmul(ps[:, 5 + bank, KEYS * n:KEYS * n + KEYS],
                                              q_bd[:, u, :, :].rearrange("p r m -> p (r m)"),
                                              k_h[:, i, TH * a:TH * a + KH, TW * b:TW * b + KW],
                                              start=False, stop=(n == UPB - 1), skip_group_check=True)
                mm.then_inc(g_s.sem, 1)

            def window_out(pair):
                pe.wait_ge(g_sm.sem, g_sm.done(pair))
                pe.wait_ge(g_v_sb.sem, g_v_sb.done(pair))
                for t in range(UNITS // 2):
                    mm = nc.tensor.transpose(ps[:, (7, 4)[t // 4], P * (t % 4):P * (t % 4) + P],
                                             prob[:, 2 * t:2 * t + 2, :].rearrange("p u k -> p (u k)"),
                                             kc[:, K_ID:K_ID + P])
                    if t % 4 == 3:
                        mm.then_inc(g_t.sem, 1)
                alone(pe)
                pe.wait_ge(g_t_sb.sem, g_t_sb.done(pair))
                for u in range(UNITS):
                    i, a, b = u // (TA * TB), u // TB % TA, u % TB
                    half, t = u % 2, u // 2
                    keys = slice(KSLOT * half, KSLOT * half + KEYS)
                    for r in range(R):
                        o = ps[C * r:C * r + C, 5 + half, :].rearrange("p (i y x) -> p i y x", i=2, x=W)
                        mm = nc.tensor.matmul(o[:, i, TH * a:TH * a + TH, TW * b:TW * b + TW],
                                              v_t[keys, t, C * r:C * r + C],
                                              p_t[keys, t, TH * TW * r:TH * TW * r + TH * TW],
                                              start=True, stop=True)
                mm.then_inc(g_pv.sem, 1)

            def one(pair):
                qkv(pair)
                gram(pair)
                by_head(pair)
                attn_out(pair)
                gate_info(pair)
                reduce_1(pair)
                conv1(pair)
                averages(pair)
                conv2(pair)
                window_qkv(pair)
                window_scores(pair)
                window_out(pair)

            with pe.Fori(0, PAIRS) as pair:
                one(pair)


def shape_constants():
    import numpy as np
    p = np.arange(P)
    c = np.zeros((P, K_END), np.float32)
    c[:, K_EQ:K_EQ + C] = p[:, None] % C == np.arange(C)
    c[:, K_HEAD:K_HEAD + P] = (p[:, None] // C == p // C) & (p[:, None] % C // D == p % C // D)
    c[:, K_SELJ:K_SELJ + R] = p[:, None] % D == np.arange(R)
    c[:, K_AVG:K_AVG + P] = (p[:, None] % C == p % C) / R
    c[:, K_ID:K_ID + P] = np.eye(P)
    y, x = p[:, None] % (TH * TW) // TW, p[:, None] % TW
    ky, kx = np.arange(KEYS) // KW, np.arange(KEYS) % KW
    near = (ky >= y) & (ky <= y + 2) & (kx >= x) & (kx <= x + 2)
    c[:, K_WIN:K_END] = np.tile(np.where(near, 0.0, -1e30), (1, UPB))
    return c


def kernel(**inputs):
    import numpy as np
    import concourse.bacc as bacc
    from concourse.bass_utils import run_bass_kernel_spmd

    a = {k: np.asarray(v) for k, v in inputs.items()}
    L0 = {k[8:]: v for k, v in a.items() if k.startswith("L0_conv_")}
    L1 = {k[8:]: v for k, v in a.items() if k.startswith("L1_conv_")}

    def by_partition(v):
        return np.tile(v.reshape(C, 1), (R, 1))

    def spread_row(v):
        return np.tile(v.reshape(1, -1), (P, 1))

    def taps(w):
        return w.transpose(3, 1, 2, 0)

    o_rows = L0["o_w"].reshape(C, C // D, D).transpose(1, 2, 0)
    o_rows = np.tile(np.repeat(o_rows.reshape(C // D, D * C), D, axis=0), (R, 1))
    arrays = {
        "x": a["x"],
        "shape_consts": shape_constants(),
        "vectors": np.concatenate(
            [by_partition(L1[k]) for k in ("conv1_b", "conv2_b", "mask_b", "q_b", "k_b", "v_b")]
            + [spread_row(L0["scale"])]
            + [spread_row(L0[k]) for k in ("ln1_g", "ln1_b", "ln2_g", "ln2_b")] + [o_rows], axis=1),
        "w1_qkv": np.concatenate([L0[k].reshape(C, C) for k in ("q1", "k1", "v1")], axis=1),
        "w3_qkv": np.stack([taps(L0[k]) for k in ("q3", "k3", "v3")], axis=2)
                    .transpose(1, 0, 2, 3, 4).reshape(C, 3, 3, 3 * C),
        "w1_gi": np.concatenate([L0[k].reshape(EC, C) for k in ("g1", "i1")], axis=1),
        "w3_gi": np.stack([taps(L0[k]) for k in ("g3", "i3")], axis=2)
                   .transpose(1, 0, 2, 3, 4).reshape(EC, 3, 2, 3 * EC),
        "conv_w": np.stack([taps(L1[k]).reshape(3 * C, 3, C) for k in ("conv1_w", "conv2_w", "mask_w")], axis=1),
        "l1_qkv": np.stack([L1[k].reshape(C, C).T for k in ("q_w", "k_w", "v_w")], axis=1),
        "r1_t": L0["r1"].reshape(C, EC).T,
    }
    nc = bacc.Bacc("TRN2", target_bir_lowering=False, num_devices=1)
    feed, args = {}, []
    for name, v in arrays.items():
        v = np.ascontiguousarray(v)
        feed[f"in_{name}"] = v
        args.append(nc.dram_tensor(f"in_{name}", v.shape, mybir.dt.from_np(v.dtype), kind="ExternalInput").ap())
    args.append(nc.dram_tensor("out_x", (B, C, H, W), F32, kind="ExternalOutput").ap())
    build(nc, *args)
    return run_bass_kernel_spmd(nc, [feed], core_ids=[0]).results[0]["out_x"]
```

```python
from contextlib import ExitStack

import concourse.bass as bass
from concourse import mybir

F32 = mybir.dt.float32
BF16 = mybir.dt.bfloat16
ALU = mybir.AluOpType
ACT = mybir.ActivationFunctionType
AX = mybir.AxisListType

P = 128
B, C, H, W = 8, 32, 32, 32
PAIRS = B // 2
R = P // C
RH = H // R
BLK = RH * W
PW = W + 2
PLANE = (H + 2) * W
D = 4
EC = 64
EPS = 1e-5
SLOPE = 0.2
BANK = 512

TH, TW = 4, 8
KH, KW = TH + 2, TW + 2
KEYS = KH * KW
TA, TB = RH // TH, W // TW
UNITS = 2 * TA * TB
UPB = UNITS // 2
KSLOT = 64

GI_BANKS = (1, 3, 2, 0)

K_EQ, K_HEAD, K_SELJ, K_AVG, K_ID, K_WIN = 0, 32, 160, 164, 292, 420
K_END = K_WIN + UPB * KEYS
V_BC1, V_BC2, V_BM, V_BQ, V_BK, V_BV, V_SCALE, V_LN, V_OW = 0, 1, 2, 3, 4, 5, 6, 7, 7 + 4 * W
V_END = V_OW + D * C


class Signal:

    def __init__(self, sem, per_pair, start):
        self.sem, self.per_pair, self.start = sem, per_pair, start

    def at(self, pair, k):
        assert k or self.start, self.sem
        return pair * self.per_pair + (k + self.start)

    def before(self, pair):
        return self.at(pair, 0)

    def done(self, pair):
        return self.at(pair, self.per_pair)


def build(nc, x, shape_consts, vectors, w1_qkv, w3_qkv, w1_gi, w3_gi, conv_w, l1_qkv, r1_t, out):
    with ExitStack() as ctx:
        def sb(name, shape, dt=F32):
            return ctx.enter_context(nc.sbuf_tensor(name, shape, dt))

        def sem(name):
            return ctx.enter_context(nc.semaphore(name))

        signals = []

        def signal(name, per_pair, start=0):
            signals.append(Signal(sem(name), per_pair, start))
            return signals[-1]

        ps = ctx.enter_context(nc.psum_tensor("ps", [P, 8, BANK], F32))

        kc = sb("kc", [P, K_END])
        vec = sb("vec", [P, V_END])
        w1a = sb("w1a", [C, 3 * C])
        w3a = sb("w3a", [C, 3, 3, 3 * C])
        w1b = sb("w1b", [EC, 2 * C])
        w3b = sb("w3b", [EC, 3, 2, 3 * EC])
        w_conv = sb("w_conv", [P, 3, 3, C])
        w_qk = sb("w_qk", [P, 3, 2, 2, C])
        w_v = sb("w_v", [P, 3, C])
        w_gi = sb("w_gi", [3 * C, 3, 2, EC])
        w_bd = sb("w_bd", [P, 3, P])
        w_r1 = sb("w_r1", [P, 2, C])
        ident_bf = sb("ident_bf", [P, P], BF16)
        win_bf = sb("win_bf", [P, UPB * KEYS], BF16)
        inv_scale = sb("inv_scale", [P, 1])
        half_bm = sb("half_bm", [P, 1])
        ones = sb("ones", [P, 2 * BLK])
        neg_half = sb("neg_half", [P, 2 * RH])

        x_in = sb("x_in", [P, 2, BLK])
        x1 = sb("x1", [P, 2, BLK])
        x2 = sb("x2", [P, 2, BLK])
        out_s = sb("out_s", [P, 2, BLK])
        ln1_out = sb("ln1_out", [P, 2, BLK])
        ln2_out = sb("ln2_out", [P, 2, BLK])
        act_in = sb("act_in", [P, 2, BLK])
        sh_ln1 = sb("sh_ln1", [P, 2, PLANE])
        sh_ln2 = sb("sh_ln2", [3 * C, 2, PLANE])
        sh_x2 = sb("sh_x2", [P, 2, PLANE])
        sh_in = sb("sh_in", [P, 2, PLANE])
        ln_c = sb("ln_c", [P, 2 * RH, W])
        ln_q = sb("ln_q", [P, 2 * RH, W])
        ln_s = sb("ln_s", [P, 4, 2 * RH])
        qk_t = sb("qk_t", [P, 2, BANK])
        v4 = sb("v4", [P, 2, BLK])
        sc_m = sb("sc_m", [P, 2 * D, C])
        sc_d = sb("sc_d", [P, 2 * D])
        sm = sb("sm", [P, 4, 2 * D])
        mix_p = sb("mix_p", [P, 2, D, C])
        mix_s = sb("mix_s", [P, 2, C])
        mix = sb("mix", [P, 2, R, C])
        gate = sb("gate", [P, 4, BANK])
        gi = sb("gi", [P, 2, BANK])
        hn = sb("hn", [P, 2, BLK])
        hc = sb("hc", [P, 2, BLK])
        st6 = sb("st6", [P, 2, 6])
        st = sb("st", [P, 2, 2])
        sts = sb("sts", [P, 8, 2])
        th = sb("th", [P, 2 * BLK])
        msk = sb("msk", [P, 2 * BLK])
        omm = sb("omm", [P, 2 * BLK])
        xm = sb("xm", [P, 2, RH + 2, PW])
        q_bd = sb("q_bd", [P, UNITS, R, TH * TW])
        k_h = sb("k_h", [P, 2, RH + 2, PW])
        xw = sb("xw", [P, UNITS, KEYS])
        v_t = sb("v_t", [P, UNITS // 2, P])
        prob = sb("prob", [P, UNITS, KSLOT])
        wsm = sb("wsm", [P, 3, UNITS])
        p_t = sb("p_t", [P, UNITS // 2 * R, 2, TH * TW])
        out1 = sb("out1", [P, 2 * BLK])
        res = sb("res", [P, 2 * BLK])
        dif = sb("dif", [P, 2 * BLK])

        s_consts, s_w, s_diag = sem("s_consts"), sem("s_w"), sem("s_diag")
        s_zero, s_zero_bd = sem("s_zero"), sem("s_zero_bd")
        s_fold, s_wready = sem("s_fold"), sem("s_wready")

        g_x = signal("x_loaded", 16 * R)
        g_ln = [signal("ln1_steps", 8), signal("ln2_steps", 8)]
        g_sq = [signal("ln1_squares", 1), signal("ln2_squares", 1)]
        g_rs = [signal("ln1_rstd", 1), signal("ln2_rstd", 1)]
        planes_by = {n: [signal(f"{n}_planes_dma", 16 * R, start=1), signal(f"{n}_planes_dve", 1, start=1),
                         signal(f"{n}_planes_act", 1, start=1)] for n in ("ln1", "ln2", "x2", "in")}
        g_qkt = signal("qkt_in_psum", 2)
        g_qkt_sb = signal("qkt_in_sbuf", 2)
        g_v4 = signal("v4_in_psum", 1, start=1)
        g_v4_sb = signal("v4_in_sbuf", 1)
        g_gram = signal("gram_in_psum", 1, start=1)
        g_score = signal("score_steps", 11)
        g_rep = signal("scores_by_head", 1)
        g_pexp = signal("head_exp", 1)
        g_y = signal("attn_out_in_psum", 1, start=1)
        g_x1 = signal("x1_done", 1)
        g_i = signal("gate_info_in_psum", 4, start=1)
        g_gelu = signal("gelu_done", 4)
        g_gi = signal("gated", 4, start=1)
        g_r1 = signal("r1_in_psum", 1, start=1)
        g_x2 = signal("x2_done", 1, start=1)
        g_xw = signal("key_windows", 2 * TA)
        g_c1 = signal("conv1_in_psum", 1, start=1)
        g_c1_sb = signal("conv1_in_sbuf", 1)
        g_in = signal("inorm_steps", 8)
        g_avg = signal("inorm_averages", 2, start=1)
        g_inr = signal("inorm_rstd", 1)
        g_act = signal("inorm_applied", 2, start=1)
        g_lr = signal("lrelu_done", 1, start=1)
        g_mk = signal("mask_in_psum", 1)
        g_c2 = signal("conv2_in_psum", 1, start=1)
        g_th = signal("tanh_done", 1)
        g_xm = signal("masked_steps", 2, start=1)
        g_halo = signal("halo_loaded", 2 * 16, start=1)
        g_q = signal("q_in_psum", 1)
        g_k = signal("k_in_psum", 1)
        g_v = signal("v_in_psum", 1, start=1)
        g_q_sb = signal("q_in_sbuf", 4)
        g_k_sb = signal("k_in_sbuf", 2)
        g_v_sb = signal("v_in_sbuf", 2)
        g_s = signal("sims_in_psum", 1, start=1)
        g_sm = signal("window_softmax_steps", 5)
        g_we = signal("window_exp", 1)
        g_t = signal("probs_t_in_psum", 2, start=1)
        g_t_sb = signal("probs_t_in_sbuf", 4, start=1)
        g_pv = signal("window_out_in_psum", 1, start=1)
        g_o1 = signal("out1_in_sbuf", 1)
        g_res = signal("residual_steps", 2, start=1)
        g_fin = signal("final_steps", 3, start=1)
        g_out = signal("out_stored", 16 * R, start=1)

        block = ctx.enter_context(nc.Block())

        x_dram = x.rearrange("b c (r q) w -> r c b (q w)", r=R)
        out_dram = out.rearrange("b c (r q) w -> r c b (q w)", r=R)

        def alone(engine):
            engine.wait_ge(s_zero, Z_PADS)

        def flat(t):
            return t.rearrange("p i m -> p (i m)")

        def plane(t):
            return t[:, :, :].rearrange("p i (y x) -> p i y x", x=W)

        def shift_copies(copy, src, planes, s, last):
            cut_left, cut_right = max(1 - s, 0), max(s - 1, 0)
            n = W - cut_left - cut_right
            for r in range(R):
                rows = slice(C * r, C * r + C)
                ins = copy(plane(planes)[C * s:C * s + C, :, 1 + RH * r:1 + RH * r + RH, cut_left:cut_left + n],
                           src[rows, :, :].rearrange("p i (y x) -> p i y x", x=W)
                           [:, :, :, cut_right:cut_right + n])
            if last:
                ins.then_inc(last.sem, 1)

        Z_PADS = 7

        @block.sync
        def _(sp):
            def load_x(pair):
                for r in range(R):
                    sp.dma_start(x_in[C * r:C * r + C, :, :],
                                 x_dram[r][:, bass.ts(pair, 2), :]).then_inc(g_x.sem, 16)

            def spread(src, planes, done):
                for r in range(R):
                    start = (1 + RH * r) * W
                    sp.dma_start(planes[C:2 * C, :, start:start + BLK], src[C * r:C * r + C]).then_inc(done.sem, 16)

            load_x(0)
            sp.dma_start(vec[:, :], vectors).then_inc(s_consts, 16)
            sp.dma_start(w1a[:, :], w1_qkv).then_inc(s_w, 16)
            sp.dma_start(w3a[:, :, :, :], w3_qkv).then_inc(s_w, 16)
            sp.dma_start(w1b[:, :], w1_gi).then_inc(s_w, 16)
            sp.dma_start(w3b[:, :, :, :], w3_gi).then_inc(s_w, 16)
            for g in signals:
                if g.start:
                    sp.sem_inc(g.sem, g.start)
            sp.wait_ge(s_zero, Z_PADS)

            def ln1_planes(pair):
                sp.wait_ge(g_v4.sem, g_v4.before(pair))
                sp.wait_ge(g_ln[0].sem, g_ln[0].done(pair))
                spread(ln1_out, sh_ln1, planes_by["ln1"][0])

            def ln2_planes(pair):
                sp.wait_ge(g_ln[1].sem, g_ln[1].done(pair))
                sp.wait_ge(g_i.sem, g_i.before(pair))
                spread(ln2_out, sh_ln2, planes_by["ln2"][0])

            def x2_planes(pair):
                sp.wait_ge(g_x2.sem, g_x2.done(pair))
                alone(sp)
                sp.wait_ge(g_c1.sem, g_c1.before(pair))
                spread(x2, sh_x2, planes_by["x2"][0])

            def in_planes(pair):
                alone(sp)
                sp.wait_ge(g_lr.sem, g_lr.done(pair))
                spread(act_in, sh_in, planes_by["in"][0])

            def halo(pair):
                sp.wait_ge(g_xm.sem, g_xm.at(pair, 2))
                sp.dma_start(xm[C:P, :, 0, :], xm[0:P - C, :, RH, :]).then_inc(g_halo.sem, 16)
                sp.dma_start(xm[0:P - C, :, RH + 1, :], xm[C:P, :, 1, :]).then_inc(g_halo.sem, 16)

            def store(pair):
                alone(sp)
                sp.wait_ge(g_fin.sem, g_fin.done(pair))
                for r in range(R):
                    sp.dma_start(out_dram[r][:, bass.ts(pair, 2), :], out_s[C * r:C * r + C, :, :])\
                      .then_inc(g_out.sem, 16)

            def load_next(pair):
                alone(sp)
                sp.wait_ge(g_x1.sem, g_x1.done(pair))
                load_x(pair + 1)

            def step(pair, more):
                in_planes(pair)
                if more:
                    load_next(pair + 1)
                ln2_planes(pair + 1)
                halo(pair)
                x2_planes(pair + 1)
                if more:
                    ln1_planes(pair + 2)
                store(pair)

            ln1_planes(0)
            load_next(0)
            ln2_planes(0)
            x2_planes(0)
            ln1_planes(1)
            with sp.Fori(0, PAIRS - 2) as pair:
                step(pair, True)
            step(PAIRS - 2, False)
            in_planes(PAIRS - 1)
            halo(PAIRS - 1)
            store(PAIRS - 1)
            sp.wait_ge(g_out.sem, g_out.done(PAIRS - 1))

        @block.gpsimd
        def _(pool):
            for t in (sh_ln1, sh_ln2, sh_x2, sh_in, xm):
                nc.gpsimd.memset(t[:], 0.0).then_inc(s_zero, 1)
            nc.gpsimd.memset(neg_half[:, :], -0.5).then_inc(s_zero, 1)
            nc.gpsimd.memset(ones[:, :], 1.0).then_inc(s_zero, 1)
            pool.wait_ge(s_zero, Z_PADS)

            def rstd(g, rs, pair):
                pool.wait_ge(g.sem, g.at(pair, 5))
                nc.gpsimd.tensor_tensor(ln_s[:, 3, :], ln_s[:, 2, :], neg_half[:, :], ALU.pow)\
                  .then_inc(rs.sem, 1)

            def inorm_rstd(pair):
                pool.wait_ge(g_in.sem, g_in.at(pair, 6))
                nc.gpsimd.tensor_tensor(sts[:, 6, :], sts[:, 4, :], neg_half[:, 0:2], ALU.pow)\
                  .then_inc(g_inr.sem, 1)

            def residual(pair):
                pool.wait_ge(g_xm.sem, g_xm.at(pair, 1))
                pool.wait_ge(g_fin.sem, g_fin.before(pair))
                nc.gpsimd.tensor_tensor(omm[:, :], ones[:, :], msk[:, :], ALU.subtract)\
                  .then_inc(g_res.sem, 1)
                pool.wait_ge(g_o1.sem, g_o1.done(pair))
                pool.wait_ge(g_x2.sem, g_x2.done(pair))
                nc.gpsimd.tensor_tensor(res[:, :], out1[:, :], flat(x2[:, :, :]), ALU.add)\
                  .then_inc(g_res.sem, 1)

            def step(pair, more):
                inorm_rstd(pair)
                rstd(g_ln[1], g_rs[1], pair + 1)
                residual(pair)
                if more:
                    rstd(g_ln[0], g_rs[0], pair + 2)

            rstd(g_ln[0], g_rs[0], 0)
            rstd(g_ln[1], g_rs[1], 0)
            rstd(g_ln[0], g_rs[0], 1)
            with pool.Fori(0, PAIRS - 2) as pair:
                step(pair, True)
            step(PAIRS - 2, False)
            inorm_rstd(PAIRS - 1)
            residual(PAIRS - 1)

        @block.scalar
        def _(act):
            act.dma_start(kc[:, :], shape_consts).then_inc(s_consts, 16)
            act.wait_ge(s_zero_bd, 3)
            act.dma_start(w_conv[0:3 * C, :, :, :], conv_w).then_inc(s_diag, 16)
            for r in range(R):
                act.dma_start(w_bd[C * r:C * r + C, :, C * r:C * r + C], l1_qkv).then_inc(s_diag, 16)
            for h in range(2):
                act.dma_start(w_r1[EC * h:EC * h + EC, h, :], r1_t).then_inc(s_diag, 16)

            def squares(g, sq, pair):
                act.wait_ge(g.sem, g.at(pair, 3))
                nc.scalar.activation(ln_q[:, :, :], ln_c[:, :, :], ACT.Square).then_inc(sq.sem, 1)

            def act_copy(o, i):
                return nc.scalar.activation(o, i, ACT.Copy)

            def planes(name, src, dst, src_ready, reader, pair):
                act.wait_ge(src_ready.sem, src_ready.done(pair))
                act.wait_ge(reader.sem, reader.before(pair))
                shift_copies(act_copy, src, dst, 2, planes_by[name][2])

            def front_qkv(pair):
                for i in range(2):
                    act.wait_ge(g_qkt.sem, g_qkt.at(pair, i + 1))
                    act.wait_ge(g_gram.sem, g_gram.before(pair))
                    nc.scalar.activation(qk_t[:, i, :], ps[:, i, :], ACT.Copy).then_inc(g_qkt_sb.sem, 1)
                act.wait_ge(g_v4.sem, g_v4.done(pair))
                act.wait_ge(g_y.sem, g_y.before(pair))
                nc.scalar.activation(v4[:, :, :].rearrange("p i m -> p (i m)"), ps[:, 2, :], ACT.Copy)\
                  .then_inc(g_v4_sb.sem, 1)

            def head_exp(pair):
                act.wait_ge(g_score.sem, g_score.at(pair, 5))
                nc.scalar.activation(sm[:, 2, :], sm[:, 1, :], ACT.Exp).then_inc(g_pexp.sem, 1)

            def gelu(pair, n):
                act.wait_ge(g_i.sem, g_i.at(pair, n + 1))
                act.wait_ge(g_gi.sem, g_gi.before(pair))
                nc.scalar.activation(gate[EC:P, n, :], ps[0:EC, GI_BANKS[n], :], ACT.Gelu).then_inc(g_gelu.sem, 1)

            def conv1_evac(pair):
                act.wait_ge(g_c1.sem, g_c1.done(pair))
                act.wait_ge(g_act.sem, g_act.before(pair))
                nc.scalar.activation(hc[:, :, :].rearrange("p i m -> p (i m)"), ps[:, 4, :], ACT.Identity,
                                     bias=vec[:, V_BC1:V_BC1 + 1]).then_inc(g_c1_sb.sem, 1)

            def inorm_apply(pair):
                act.wait_ge(g_in.sem, g_in.done(pair))
                act.wait_ge(g_lr.sem, g_lr.before(pair))
                for i in range(2):
                    nc.scalar.activation(hn[:, i, :], hc[:, i, :], ACT.Identity,
                                         bias=sts[:, 7, i:i + 1], scale=sts[:, 6, i:i + 1])\
                      .then_inc(g_act.sem, 1)

            def tanh_mask(pair):
                act.wait_ge(g_mk.sem, g_mk.done(pair))
                act.wait_ge(g_xm.sem, g_xm.before(pair))
                act.wait_ge(g_res.sem, g_res.before(pair))
                nc.scalar.activation(th[:, :], ps[:, 6, :], ACT.Tanh, bias=half_bm[:, 0:1], scale=0.5)\
                  .then_inc(g_th.sem, 1)

            def out1_evac(pair):
                act.wait_ge(g_c2.sem, g_c2.done(pair))
                act.wait_ge(g_fin.sem, g_fin.before(pair))
                act.wait_ge(g_res.sem, g_res.before(pair))
                nc.scalar.activation(out1[:, :], ps[:, 7, :], ACT.Identity, bias=vec[:, V_BC2:V_BC2 + 1])\
                  .then_inc(g_o1.sem, 1)

            def qk_evac(pair):
                act.wait_ge(g_q.sem, g_q.done(pair))
                act.wait_ge(g_s.sem, g_s.before(pair))
                for r in range(R):
                    rows = slice(C * r, C * r + C)
                    nc.scalar.activation(q_bd[rows, :, r, :],
                                         ps[rows, 4, :].rearrange("p (u m) -> p u m", u=UNITS), ACT.Identity,
                                         bias=vec[rows, V_BQ:V_BQ + 1]).then_inc(g_q_sb.sem, 1)
                act.wait_ge(g_k.sem, g_k.done(pair))
                for i in range(2):
                    nc.scalar.activation(k_h[:, i, :, :].rearrange("p y x -> p (y x)"),
                                         ps[:, 5 + i, 0:(RH + 2) * PW], ACT.Identity,
                                         bias=vec[:, V_BK:V_BK + 1]).then_inc(g_k_sb.sem, 1)

            def key_windows(pair):
                act.wait_ge(g_halo.sem, g_halo.done(pair))
                act.wait_ge(g_v.sem, g_v.before(pair))
                for ia in range(2 * TA):
                    i, a = ia // TA, ia % TA
                    for b in range(TB):
                        ins = nc.scalar.activation(
                            xw[:, TB * ia + b, :].rearrange("p (y x) -> p y x", x=KW),
                            xm[:, i, TH * a:TH * a + KH, TW * b:TW * b + KW], ACT.Copy)
                    ins.then_inc(g_xw.sem, 1)

            def window_exp(pair):
                act.wait_ge(g_sm.sem, g_sm.at(pair, 2))
                nc.scalar.activation(prob[:, :, 0:KEYS], prob[:, :, 0:KEYS], ACT.Exp).then_inc(g_we.sem, 1)

            def probs_t(pair):
                act.wait_ge(g_pv.sem, g_pv.before(pair))
                for t in range(2):
                    act.wait_ge(g_t.sem, g_t.at(pair, t + 1))
                    for h in range(2):
                        rows = slice(KSLOT * h, KSLOT * h + KSLOT)
                        nc.scalar.activation(p_t[rows, 4 * R * t:4 * R * t + 4 * R, h, :],
                                             ps[rows, (7, 4)[t], :].rearrange("p (q m) -> p q m", m=TH * TW),
                                             ACT.Copy).then_inc(g_t_sb.sem, 1)

            act.wait_ge(s_consts, 32)
            act.wait_ge(s_wready, 8)

            def ln1(pair):
                squares(g_ln[0], g_sq[0], pair)
                planes("ln1", ln1_out, sh_ln1, g_ln[0], g_v4, pair)

            def ln2(pair):
                squares(g_ln[1], g_sq[1], pair)
                planes("ln2", ln2_out, sh_ln2, g_ln[1], g_i, pair)

            def x2_planes(pair):
                planes("x2", x2, sh_x2, g_x2, g_c1, pair)

            def in_planes(pair):
                planes("in", act_in, sh_in, g_lr, g_c2, pair)

            def step(pair, more):
                front_qkv(pair + 1)
                conv1_evac(pair)
                head_exp(pair + 1)
                inorm_apply(pair)
                in_planes(pair)
                ln2(pair + 1)
                tanh_mask(pair)
                out1_evac(pair)
                qk_evac(pair)
                key_windows(pair)
                for n in range(4):
                    gelu(pair + 1, n)
                window_exp(pair)
                x2_planes(pair + 1)
                probs_t(pair)
                if more:
                    ln1(pair + 2)

            ln1(0)
            front_qkv(0)
            head_exp(0)
            ln2(0)
            for n in range(4):
                gelu(0, n)
            x2_planes(0)
            ln1(1)
            with act.Fori(0, PAIRS - 2) as pair:
                step(pair, True)
            step(PAIRS - 2, False)
            last = PAIRS - 1
            conv1_evac(last)
            inorm_apply(last)
            in_planes(last)
            tanh_mask(last)
            out1_evac(last)
            qk_evac(last)
            key_windows(last)
            window_exp(last)
            probs_t(last)

        @block.vector
        def _(dve):
            for t in (w_bd, w_r1, w_conv):
                nc.vector.memset(t[:], 0.0).then_inc(s_zero_bd, 1)
            for t in (ps, q_bd, prob, p_t):
                nc.vector.memset(t[:], 0.0).then_inc(s_zero_bd, 1)
            dve.wait_ge(s_consts, 32)
            nc.vector.tensor_copy(ident_bf[:, :], kc[:, K_ID:K_ID + P]).then_inc(s_wready, 1)
            nc.vector.tensor_copy(win_bf[:, :], kc[:, K_WIN:K_END]).then_inc(s_wready, 1)
            nc.vector.reciprocal(inv_scale[:, :], vec[:, V_SCALE:V_SCALE + 1]).then_inc(s_wready, 1)
            nc.vector.tensor_scalar(half_bm[:, :], vec[:, V_BM:V_BM + 1], 0.5, None, ALU.mult)\
              .then_inc(s_wready, 1)
            dve.wait_ge(s_fold, 2)
            qk_f = ps[:, 0, 0:12 * C].rearrange("p (d m y o) -> p d m y o", d=2, m=2, o=C)
            for d in range(2):
                nc.vector.tensor_copy(w_qk[:, :, d, :, :].rearrange("p y m o -> p m y o"), qk_f[:, d])\
                  .then_inc(s_wready, 1)
            nc.vector.tensor_copy(w_v[:, :, :], ps[:, 2, 0:3 * C].rearrange("p (y o) -> p y o", o=C))\
              .then_inc(s_wready, 1)
            gi_f = ps[0:3 * C, 1, 0:6 * EC].rearrange("p (m y o) -> p m y o", m=2, o=EC)
            nc.vector.tensor_copy(w_gi[:, :, :, :].rearrange("p y m o -> p m y o"), gi_f).then_inc(s_wready, 1)
            dve.wait_ge(s_wready, 8)
            dve.wait_ge(s_zero, Z_PADS)

            def layernorm(n, src, dst, pair, src_ready, dst_free):
                g, sq, rs = g_ln[n], g_sq[n], g_rs[n]
                x3 = src.rearrange("p i (y x) -> p (i y) x", x=W)
                rows = 2 * RH

                def per_row(k):
                    return ln_s[:, k, :].unsqueeze(2).broadcast_to([P, rows, W])

                def per_col(k):
                    return vec[:, V_LN + W * k:V_LN + W * k + W].unsqueeze(1).broadcast_to([P, rows, W])

                src_ready()
                nc.vector.reduce_sum(ln_s[:, 0, :], x3, AX.X).then_inc(g.sem, 1)
                dve.wait_ge(g.sem, g.at(pair, 1))
                nc.vector.tensor_scalar(ln_s[:, 0, :], ln_s[:, 0, :], 1.0 / W, None, ALU.mult)\
                  .then_inc(g.sem, 1)
                dve.wait_ge(g.sem, g.at(pair, 2))
                nc.vector.tensor_tensor(ln_c[:, :, :], x3, per_row(0), ALU.subtract).then_inc(g.sem, 1)
                dve.wait_ge(sq.sem, sq.done(pair))
                nc.vector.reduce_sum(ln_s[:, 1, :], ln_q[:, :, :], AX.X).then_inc(g.sem, 1)
                dve.wait_ge(g.sem, g.at(pair, 4))
                nc.vector.tensor_scalar(ln_s[:, 2, :], ln_s[:, 1, :], 1.0 / W, EPS, ALU.mult, ALU.add)\
                  .then_inc(g.sem, 1)
                dve.wait_ge(rs.sem, rs.done(pair))
                nc.vector.tensor_tensor(ln_c[:, :, :], ln_c[:, :, :], per_row(3), ALU.mult).then_inc(g.sem, 1)
                dve.wait_ge(g.sem, g.at(pair, 6))
                nc.vector.tensor_tensor(ln_c[:, :, :], ln_c[:, :, :], per_col(2 * n), ALU.mult)\
                  .then_inc(g.sem, 1)
                dve.wait_ge(g.sem, g.at(pair, 7))
                dst_free()
                nc.vector.tensor_tensor(dst[:, :, :].rearrange("p i (y x) -> p (i y) x", x=W),
                                        ln_c[:, :, :], per_col(2 * n + 1), ALU.add).then_inc(g.sem, 1)

            def planes_read(name, pair):
                for g in (planes_by[name][0], planes_by[name][2]):
                    dve.wait_ge(g.sem, g.before(pair))

            def planes(name, src, dst, src_ready, reader, pair):
                dve.wait_ge(src_ready.sem, src_ready.done(pair))
                dve.wait_ge(reader.sem, reader.before(pair))
                if name == "ln1":
                    shift_copies(nc.vector.tensor_copy, src, dst, 3, None)
                shift_copies(nc.vector.tensor_copy, src, dst, 0, planes_by[name][1])

            def ln1(pair):
                layernorm(0, x_in[:, :, :], ln1_out, pair,
                          lambda: dve.wait_ge(g_x.sem, g_x.done(pair)),
                          lambda: planes_read("ln1", pair))

            sm3 = [sm[:, k, :].rearrange("p (i e) -> p i e", e=D) for k in range(3)]

            def per_image(col):
                return sm[:, 3, col:col + 2].unsqueeze(2).broadcast_to([P, 2, D])

            def head_scores(pair):
                g = g_score
                dve.wait_ge(g_gram.sem, g_gram.done(pair))
                eq = kc[:, K_EQ:K_EQ + C].unsqueeze(1).broadcast_to([P, 2 * D, C])
                nc.vector.tensor_tensor(sc_m[:, :, :], ps[:, 3, 0:2 * P].rearrange("p (e c) -> p e c", c=C),
                                        eq, ALU.mult).then_inc(g.sem, 1)
                dve.wait_ge(g.sem, g.at(pair, 1))
                nc.vector.reduce_sum(sc_d[:, :], sc_m[:, :, :], AX.X).then_inc(g.sem, 1)

            def head_max(pair):
                g = g_score
                dve.wait_ge(g_rep.sem, g_rep.done(pair))
                nc.vector.tensor_scalar(sm[:, 0, :], ps[:, 3, 2 * P:2 * P + 2 * D], inv_scale[:, 0:1], None,
                                        ALU.mult).then_inc(g.sem, 1)
                dve.wait_ge(g.sem, g.at(pair, 3))
                nc.vector.reduce_max(sm[:, 3, 0:2], sm3[0], AX.X).then_inc(g.sem, 1)
                dve.wait_ge(g.sem, g.at(pair, 4))
                nc.vector.tensor_tensor(sm3[1], sm3[0], per_image(0), ALU.subtract).then_inc(g.sem, 1)

            def head_mix(pair):
                g = g_score
                dve.wait_ge(g_pexp.sem, g_pexp.done(pair))
                nc.vector.reduce_sum(sm[:, 3, 2:4], sm3[2], AX.X).then_inc(g.sem, 1)
                dve.wait_ge(g.sem, g.at(pair, 6))
                nc.vector.reciprocal(sm[:, 3, 4:6], sm[:, 3, 2:4]).then_inc(g.sem, 1)
                dve.wait_ge(g.sem, g.at(pair, 7))
                nc.vector.tensor_tensor(sm3[0], sm3[2], per_image(4), ALU.mult).then_inc(g.sem, 1)
                dve.wait_ge(g.sem, g.at(pair, 8))
                for i in range(2):
                    p_b = sm[:, 0, D * i:D * i + D].unsqueeze(2).broadcast_to([P, D, C])
                    ow = vec[:, V_OW:V_OW + D * C].rearrange("p (e o) -> p e o", o=C)
                    mul = nc.vector.tensor_tensor(mix_p[:, i, :, :], ow, p_b, ALU.mult)
                mul.then_inc(g.sem, 1)
                dve.wait_ge(g.sem, g.at(pair, 9))
                nc.vector.reduce_sum(mix_s[:, :, :], mix_p[:, :, :, :].rearrange("p i e o -> p i o e"), AX.X)\
                  .then_inc(g.sem, 1)
                dve.wait_ge(g.sem, g.at(pair, 10))
                sel = kc[:, K_SELJ:K_SELJ + R].unsqueeze(2).broadcast_to([P, R, C])
                for i in range(2):
                    mul = nc.vector.tensor_tensor(mix[:, i, :, :], sel,
                                                  mix_s[:, i, :].unsqueeze(1).broadcast_to([P, R, C]), ALU.mult)
                mul.then_inc(g.sem, 1)

            def ln2(pair):
                def x1_sum():
                    dve.wait_ge(g_y.sem, g_y.done(pair))
                    nc.vector.tensor_tensor(flat(x1[:, :, :]), ps[:, 0, :], flat(x_in[:, :, :]), ALU.add)\
                      .then_inc(g_x1.sem, 1)
                    dve.wait_ge(g_x1.sem, g_x1.done(pair))
                layernorm(1, x1[:, :, :], ln2_out, pair, x1_sum,
                          lambda: planes_read("ln2", pair))

            def gated(pair, n):
                dve.wait_ge(g_gelu.sem, g_gelu.at(pair, n + 1))
                dve.wait_ge(g_r1.sem, g_r1.before(pair))
                nc.vector.tensor_tensor(gi[EC * (n % 2):EC * (n % 2) + EC, n // 2, :], ps[EC:P, GI_BANKS[n], :],
                                        gate[EC:P, n, :], ALU.mult).then_inc(g_gi.sem, 1)

            def x2_sum(pair):
                dve.wait_ge(g_r1.sem, g_r1.done(pair))
                dve.wait_ge(g_res.sem, g_res.before(pair))
                planes_read("x2", pair)
                nc.vector.tensor_tensor(flat(x2[:, :, :]), ps[:, 1, :], flat(x1[:, :, :]),
                                        ALU.add)\
                  .then_inc(g_x2.sem, 1)

            def inorm(pair):
                g = g_in
                dve.wait_ge(g_c1_sb.sem, g_c1_sb.done(pair))
                dve.wait_ge(g_avg.sem, g_avg.before(pair))
                for i in range(2):
                    ins = nc.vector.bn_stats(st6[:, i, :], hc[:, i, :])
                ins.then_inc(g.sem, 1)
                dve.wait_ge(g.sem, g.at(pair, 1))
                nc.vector.memset(sts[:, 3, :], 0.0)
                for i in range(2):
                    ins = nc.vector.bn_aggr(st[:, i, :], st6[:, i, :])
                ins.then_inc(g.sem, 1)

            def inorm_mean(pair):
                g = g_in
                dve.wait_ge(g_avg.sem, g_avg.at(pair, 1))
                nc.vector.tensor_copy(sts[:, 0, :], ps[:, 5, 0:2]).then_inc(g.sem, 1)
                dve.wait_ge(g.sem, g.at(pair, 3))
                nc.vector.tensor_tensor(sts[:, 1, :], st[:, :, 0], sts[:, 0, :], ALU.subtract).then_inc(g.sem, 1)
                dve.wait_ge(g.sem, g.at(pair, 4))
                for i in range(2):
                    ins = nc.vector.scalar_tensor_tensor(
                        out=sts[:, 2, i:i + 1], in0=sts[:, 1, i:i + 1], scalar=sts[:, 1, i:i + 1],
                        in1=st[:, i, 1:2], op0=ALU.mult, op1=ALU.add)
                ins.then_inc(g.sem, 1)

            def inorm_var(pair):
                g = g_in
                dve.wait_ge(g_avg.sem, g_avg.at(pair, 2))
                nc.vector.tensor_scalar(sts[:, 4, :], ps[:, 5, 2:4], EPS, None, ALU.add).then_inc(g.sem, 1)
                dve.wait_ge(g_inr.sem, g_inr.done(pair))
                for i in range(2):
                    ins = nc.vector.scalar_tensor_tensor(
                        out=sts[:, 7, i:i + 1], in0=sts[:, 0, i:i + 1], scalar=-1.0,
                        in1=sts[:, 6, i:i + 1], op0=ALU.mult, op1=ALU.mult)
                ins.then_inc(g.sem, 2)

            def lrelu(pair):
                dve.wait_ge(g_c2.sem, g_c2.before(pair))
                dve.wait_ge(g_act.sem, g_act.done(pair))
                planes_read("in", pair)
                dve.wait_ge(g_xm.sem, g_xm.before(pair))
                nc.vector.scalar_tensor_tensor(out=flat(act_in[:, :, :]), in0=flat(hn[:, :, :]), scalar=SLOPE,
                                               in1=flat(hn[:, :, :]), op0=ALU.mult, op1=ALU.max)\
                  .then_inc(g_lr.sem, 1)

            def masked(pair):
                dve.wait_ge(g_th.sem, g_th.done(pair))
                nc.vector.tensor_scalar(msk[:, :], th[:, :], 0.5, 0.5, ALU.mult, ALU.add).then_inc(g_xm.sem, 1)
                dve.wait_ge(g_xm.sem, g_xm.at(pair, 1))
                dve.wait_ge(g_v.sem, g_v.before(pair))
                dve.wait_ge(g_halo.sem, g_halo.before(pair))
                nc.vector.tensor_tensor(xm[:, :, 1:1 + RH, 1:1 + W],
                                        msk[:, :].rearrange("p (i y x) -> p i y x", i=2, x=W),
                                        act_in[:, :, :].rearrange("p i (y x) -> p i y x", x=W), ALU.mult).then_inc(g_xm.sem, 1)

            def v_evac(pair):
                dve.wait_ge(g_v.sem, g_v.done(pair))
                dve.wait_ge(g_pv.sem, g_pv.before(pair))
                for h in range(2):
                    nc.vector.tensor_copy(v_t[:, 4 * h:4 * h + 4, :].rearrange("p u m -> p (u m)"),
                                          ps[:, (7, 4)[h], :]).then_inc(g_v_sb.sem, 1)

            def window_softmax(pair):
                g = g_sm
                sims = ps[:, 5:7, 0:UPB * KEYS].rearrange("p b (u k) -> p b u k", k=KEYS)
                pr4 = prob[:, :, 0:KEYS].rearrange("p (b u) k -> p b u k", b=2)

                def per_tile(k):
                    return wsm[:, k, :].unsqueeze(2).broadcast_to([P, UNITS, KEYS])

                dve.wait_ge(g_s.sem, g_s.done(pair))
                dve.wait_ge(g_t.sem, g_t.before(pair))
                nc.vector.reduce_max(wsm[:, 0, :].rearrange("p (b u) -> p b u", b=2), sims, AX.X)\
                  .then_inc(g.sem, 1)
                dve.wait_ge(g.sem, g.at(pair, 1))
                nc.vector.tensor_tensor(pr4, sims, wsm[:, 0, :].rearrange("p (b u) -> p b u", b=2)
                                        .unsqueeze(3).broadcast_to([P, 2, UPB, KEYS]), ALU.subtract)\
                  .then_inc(g.sem, 1)
                dve.wait_ge(g_we.sem, g_we.done(pair))
                nc.vector.reduce_sum(wsm[:, 1, :], prob[:, :, 0:KEYS], AX.X).then_inc(g.sem, 1)
                dve.wait_ge(g.sem, g.at(pair, 3))
                nc.vector.reciprocal(wsm[:, 2, :], wsm[:, 1, :]).then_inc(g.sem, 1)
                dve.wait_ge(g.sem, g.at(pair, 4))
                nc.vector.tensor_tensor(prob[:, :, 0:KEYS], prob[:, :, 0:KEYS], per_tile(2), ALU.mult)\
                  .then_inc(g.sem, 1)

            def final(pair):
                g = g_fin
                dve.wait_ge(g_pv.sem, g_pv.done(pair))
                dve.wait_ge(g_o1.sem, g_o1.done(pair))
                nc.vector.scalar_tensor_tensor(out=dif[:, :], in0=ps[:, 5, :], scalar=vec[:, V_BV:V_BV + 1],
                                               in1=out1[:, :], op0=ALU.add, op1=ALU.subtract).then_inc(g.sem, 1)
                dve.wait_ge(g.sem, g.at(pair, 1))
                dve.wait_ge(g_res.sem, g_res.done(pair))
                nc.vector.tensor_tensor(dif[:, :], dif[:, :], omm[:, :], ALU.mult).then_inc(g.sem, 1)
                dve.wait_ge(g.sem, g.at(pair, 2))
                dve.wait_ge(g_out.sem, g_out.before(pair))
                nc.vector.tensor_tensor(flat(out_s[:, :, :]), dif[:, :], res[:, :], ALU.add).then_inc(g.sem, 1)

            def ln1_all(pair):
                ln1(pair)
                planes("ln1", ln1_out, sh_ln1, g_ln[0], g_v4, pair)

            def ln2_all(pair):
                ln2(pair)
                planes("ln2", ln2_out, sh_ln2, g_ln[1], g_i, pair)

            def x2_all(pair):
                x2_sum(pair)
                planes("x2", x2, sh_x2, g_x2, g_c1, pair)

            def lrelu_all(pair):
                lrelu(pair)
                planes("in", act_in, sh_in, g_lr, g_c2, pair)

            def step(pair, more):
                inorm(pair)
                head_scores(pair + 1)
                inorm_mean(pair)
                head_max(pair + 1)
                inorm_var(pair)
                head_mix(pair + 1)
                lrelu_all(pair)
                ln2_all(pair + 1)
                masked(pair)
                gated(pair + 1, 0)
                gated(pair + 1, 1)
                v_evac(pair)
                gated(pair + 1, 2)
                gated(pair + 1, 3)
                window_softmax(pair)
                x2_all(pair + 1)
                if more:
                    ln1_all(pair + 2)
                final(pair)

            ln1_all(0)
            head_scores(0)
            head_max(0)
            head_mix(0)
            ln2_all(0)
            for n in range(4):
                gated(0, n)
            x2_all(0)
            ln1_all(1)
            with dve.Fori(0, PAIRS - 2) as pair:
                step(pair, True)
            step(PAIRS - 2, False)
            last = PAIRS - 1
            inorm(last)
            inorm_mean(last)
            inorm_var(last)
            lrelu_all(last)
            masked(last)
            v_evac(last)
            window_softmax(last)
            final(last)

        @block.tensor
        def _(pe):
            pe.wait_ge(s_w, 64)
            pe.wait_ge(s_zero_bd, 4)
            for d in range(2):
                for m in range(2):
                    for s in range(3):
                        at, q = 3 * C * (2 * d + m), C * (s + d)
                        nc.tensor.matmul(ps[q:q + C, 0, at:at + 3 * C], w1a[:, C * m:C * m + C],
                                         w3a[:, s, m, :], start=True, stop=True)
            for s in range(3):
                mm = nc.tensor.matmul(ps[C * s:C * s + C, 2, 0:3 * C], w1a[:, 2 * C:3 * C], w3a[:, s, 2, :],
                                      start=True, stop=True)
            mm.then_inc(s_fold, 1)
            for m in range(2):
                for s in range(3):
                    mm = nc.tensor.matmul(ps[C * s:C * s + C, 1, 3 * EC * m:3 * EC * m + 3 * EC],
                                          w1b[:, C * m:C * m + C], w3b[:, s, m, :], start=True, stop=True)
            mm.then_inc(s_fold, 1)
            pe.wait_ge(s_wready, 8)
            pe.wait_ge(s_diag, 16 * (1 + R + 2))
            pe.wait_ge(s_consts, 32)

            def block_conv(planes, bank, weight):
                for dy in range(3):
                    for r in range(R):
                        mm = nc.tensor.matmul(ps[C * r:C * r + C, bank, :], weight(dy),
                                              plane(planes)[:, :, RH * r + dy:RH * r + dy + RH, 0:W],
                                              start=(dy == 0), stop=(dy == 2))
                return mm

            def planes_ready(name, pair):
                for g in planes_by[name]:
                    pe.wait_ge(g.sem, g.done(pair))

            def qkv(pair):
                xs = plane(sh_ln1)
                planes_ready("ln1", pair)
                pe.wait_ge(g_x2.sem, g_x2.before(pair))
                for i in range(2):
                    for h in range(2):
                        for d in range(0, D, 2):
                            to = ps[:, i, 2 * P * h:2 * P * h + 2 * P]\
                                .rearrange("p (m d c) -> p d m c", m=2, d=D)[:, d:d + 2, :, :]
                            for dy in range(3):
                                at = W * (H // 2 * h + dy) + d
                                mm = nc.tensor.matmul(to, sh_ln1[:, i, at:at + D * P - D + 1:D],
                                                      w_qk[:, dy, :, :, :].rearrange("p d m c -> p (d m c)"),
                                                      start=(dy == 0), stop=(dy == 2), skip_group_check=True)
                    mm.then_inc(g_qkt.sem, 1)
                for dy in range(3):
                    for d in range(D):
                        mm = nc.tensor.matmul(ps[C * d:C * d + C, 2, :], w_v[:, dy, :],
                                              xs[:, :, dy:dy + H, d:d + W - D + 1:D],
                                              start=(dy == 0), stop=(dy == 2))
                mm.then_inc(g_v4.sem, 1)

            def gram(pair):
                for i in range(2):
                    pe.wait_ge(g_qkt_sb.sem, g_qkt_sb.at(pair, i + 1))
                    t = qk_t[:, i, :].rearrange("p (h m k) -> p h m k", h=2, m=2)
                    for h in range(2):
                        mm = nc.tensor.matmul(ps[:, 3, P * i:P * i + P], t[:, h, 1, :], t[:, h, 0, :],
                                              start=(h == 0), stop=(h == 1))
                mm.then_inc(g_gram.sem, 1)

            def by_head(pair):
                pe.wait_ge(g_score.sem, g_score.at(pair, 2))
                nc.tensor.matmul(ps[:, 3, 2 * P:2 * P + 2 * D], kc[:, K_HEAD:K_HEAD + P], sc_d[:, :],
                                 start=True, stop=True).then_inc(g_rep.sem, 1)

            def attn_out(pair):
                pe.wait_ge(g_score.sem, g_score.done(pair))
                pe.wait_ge(g_v4_sb.sem, g_v4_sb.done(pair))
                for i in range(2):
                    mm = nc.tensor.matmul(ps[:, 0, BLK * i:BLK * i + BLK],
                                          mix[:, i, :, :].rearrange("p j o -> p (j o)"), v4[:, i, :],
                                          start=True, stop=True)
                mm.then_inc(g_y.sem, 1)

            def gate_info(pair, i):
                xs = plane(sh_ln2)
                planes_ready("ln2", pair)
                pe.wait_ge(g_x1.sem, g_x1.done(pair))
                for h in range(2):
                    for dy in range(3):
                        y = H // 2 * h + dy
                        mm = nc.tensor.matmul(ps[:, GI_BANKS[2 * i + h], :],
                                              w_gi[:, dy, :, :].rearrange("p m o -> p (m o)"),
                                              xs[:, i, y:y + H // 2, 0:W], start=(dy == 0), stop=(dy == 2))
                    mm.then_inc(g_i.sem, 1)

            def reduce_1(pair):
                pe.wait_ge(g_gi.sem, g_gi.done(pair))
                for r in range(R):
                    mm = nc.tensor.matmul(ps[C * r:C * r + C, 1, :], w_r1[:, r // 2, :],
                                          gi[:, :, BLK * (r % 2):BLK * (r % 2) + BLK], start=True, stop=True)
                mm.then_inc(g_r1.sem, 1)

            def conv1(pair):
                planes_ready("x2", pair)
                pe.wait_ge(g_t_sb.sem, g_t_sb.before(pair))
                block_conv(sh_x2, 4, lambda dy: w_conv[:, 0, dy, :]).then_inc(g_c1.sem, 1)

            def average_mean(pair):
                avg = kc[:, K_AVG:K_AVG + P]
                pe.wait_ge(g_in.sem, g_in.at(pair, 2))
                pe.wait_ge(g_fin.sem, g_fin.before(pair))
                nc.tensor.matmul(ps[:, 5, 0:2], avg, st[:, :, 0], start=True, stop=True).then_inc(g_avg.sem, 1)

            def average_var(pair):
                avg = kc[:, K_AVG:K_AVG + P]
                pe.wait_ge(g_in.sem, g_in.at(pair, 5))
                nc.tensor.matmul(ps[:, 5, 2:4], avg, sts[:, 2, :], start=True, stop=True).then_inc(g_avg.sem, 1)

            def conv2(pair):
                planes_ready("in", pair)
                block_conv(sh_in, 6, lambda dy: w_conv[:, 2, dy, :]).then_inc(g_mk.sem, 1)
                block_conv(sh_in, 7, lambda dy: w_conv[:, 1, dy, :]).then_inc(g_c2.sem, 1)

            def window_qk(pair):
                pe.wait_ge(g_xm.sem, g_xm.done(pair))
                for ia in range(2 * TA):
                    i, a = ia // TA, ia % TA
                    rhs = xm[:, i, 1 + TH * a:1 + TH * a + TH, 1:1 + W]\
                        .rearrange("p y (b x) -> p b y x", x=TW)
                    mm = nc.tensor.matmul(ps[:, 4, P * ia:P * ia + P], w_bd[:, 0, :], rhs, start=True, stop=True)
                mm.then_inc(g_q.sem, 1)
                pe.wait_ge(g_halo.sem, g_halo.done(pair))
                pe.wait_ge(g_in.sem, g_in.at(pair, 6))
                pe.wait_ge(g_th.sem, g_th.done(pair))
                for i in range(2):
                    mm = nc.tensor.matmul(ps[:, 5 + i, 0:(RH + 2) * PW], w_bd[:, 1, :],
                                          xm[:, i, :, :].rearrange("p y x -> p (y x)"), start=True, stop=True)
                mm.then_inc(g_k.sem, 1)

            def window_v(pair):
                pe.wait_ge(g_o1.sem, g_o1.done(pair))
                pe.wait_ge(g_q_sb.sem, g_q_sb.done(pair))
                pe.wait_ge(g_xw.sem, g_xw.done(pair))
                for u in range(UNITS):
                    half, t = u % 2, u // 2
                    mm = nc.tensor.matmul(ps[KSLOT * half:KSLOT * half + KEYS, (7, 4)[t // 4],
                                             P * (t % 4):P * (t % 4) + P],
                                          xw[:, u, :], w_bd[:, 2, :], start=True, stop=True)
                mm.then_inc(g_v.sem, 1)

            def window_scores(pair):
                pe.wait_ge(g_k_sb.sem, g_k_sb.done(pair))
                for bank in range(2):
                    nc.tensor.matmul(ps[:, 5 + bank, 0:UPB * KEYS], ident_bf[:, :], win_bf[:, :],
                                     start=True, stop=False, skip_group_check=True)
                for r in range(0, R, 2):
                    rows = slice(C * r, C * r + 2 * C)
                    for u in range(UNITS):
                        i, a, b = u // (TA * TB), u // TB % TA, u % TB
                        at = KEYS * (u % UPB)
                        mm = nc.tensor.matmul(ps[rows, 5 + u // UPB, at:at + KEYS],
                                              q_bd[:, u, r:r + 2, :].rearrange("p r m -> p (r m)"),
                                              k_h[:, i, TH * a:TH * a + KH, TW * b:TW * b + KW],
                                              start=False, stop=(u % UPB == UPB - 1), skip_group_check=True)
                mm.then_inc(g_s.sem, 1)

            def probs_transposed(pair):
                pe.wait_ge(g_sm.sem, g_sm.done(pair))
                pe.wait_ge(g_v_sb.sem, g_v_sb.done(pair))
                for t in range(UNITS // 2):
                    mm = nc.tensor.transpose(ps[:, (7, 4)[t // 4], P * (t % 4):P * (t % 4) + P],
                                             prob[:, 2 * t:2 * t + 2, :].rearrange("p u k -> p (u k)"),
                                             kc[:, K_ID:K_ID + P])
                    if t % 4 == 3:
                        mm.then_inc(g_t.sem, 1)

            def window_out(pair):
                alone(pe)
                pe.wait_ge(g_t_sb.sem, g_t_sb.done(pair))
                for r in range(R):
                    o = ps[C * r:C * r + C, 5, :].rearrange("p (i a y b x) -> p i a b y x", i=2, a=TA, b=TB, x=TW)
                    for t in range(UNITS // 2):
                        i, a, b = t // (TA * TB // 2), t // (TB // 2) % TA, 2 * (t % (TB // 2))
                        mm = nc.tensor.matmul(o[:, i, a, b:b + 2, :, :], v_t[:, t, C * r:C * r + C],
                                              p_t[:, R * t + r, :, :].rearrange("p h m -> p (h m)"),
                                              start=True, stop=True)
                mm.then_inc(g_pv.sem, 1)

            def step(pair, more):
                qkv(pair + 1)
                conv1(pair)
                gram(pair + 1)
                average_mean(pair)
                by_head(pair + 1)
                average_var(pair)
                attn_out(pair + 1)
                conv2(pair)
                gate_info(pair + 1, 0)
                window_qk(pair)
                gate_info(pair + 1, 1)
                window_v(pair)
                window_scores(pair)
                reduce_1(pair + 1)
                probs_transposed(pair)
                window_out(pair)

            qkv(0)
            gram(0)
            by_head(0)
            attn_out(0)
            gate_info(0, 0)
            gate_info(0, 1)
            reduce_1(0)
            with pe.Fori(0, PAIRS - 2) as pair:
                step(pair, True)
            step(PAIRS - 2, False)
            last = PAIRS - 1
            conv1(last)
            average_mean(last)
            average_var(last)
            conv2(last)
            window_qk(last)
            window_v(last)
            window_scores(last)
            probs_transposed(last)
            window_out(last)


def shape_constants():
    import numpy as np
    p = np.arange(P)
    c = np.zeros((P, K_END), np.float32)
    c[:, K_EQ:K_EQ + C] = p[:, None] % C == np.arange(C)
    c[:, K_HEAD:K_HEAD + P] = (p[:, None] // C == p // C) & (p[:, None] % C // D == p % C // D)
    c[:, K_SELJ:K_SELJ + R] = p[:, None] % D == np.arange(R)
    c[:, K_AVG:K_AVG + P] = (p[:, None] % C == p % C) / R
    c[:, K_ID:K_ID + P] = np.eye(P)
    y, x = p[:, None] % (TH * TW) // TW, p[:, None] % TW
    ky, kx = np.arange(KEYS) // KW, np.arange(KEYS) % KW
    near = (ky >= y) & (ky <= y + 2) & (kx >= x) & (kx <= x + 2)
    c[:, K_WIN:K_END] = np.tile(np.where(near, 0.0, -1e30), (1, UPB))
    return c


def kernel(**inputs):
    import numpy as np
    import concourse.bacc as bacc
    from concourse.bass_utils import run_bass_kernel_spmd

    a = {k: np.asarray(v) for k, v in inputs.items()}
    L0 = {k[8:]: v for k, v in a.items() if k.startswith("L0_conv_")}
    L1 = {k[8:]: v for k, v in a.items() if k.startswith("L1_conv_")}

    def by_partition(v):
        return np.tile(v.reshape(C, 1), (R, 1))

    def spread_row(v):
        return np.tile(v.reshape(1, -1), (P, 1))

    def taps(w):
        return w.transpose(3, 1, 2, 0)

    o_rows = L0["o_w"].reshape(C, C // D, D).transpose(1, 2, 0)
    o_rows = np.tile(np.repeat(o_rows.reshape(C // D, D * C), D, axis=0), (R, 1))
    arrays = {
        "x": a["x"],
        "shape_consts": shape_constants(),
        "vectors": np.concatenate(
            [by_partition(L1[k]) for k in ("conv1_b", "conv2_b", "mask_b", "q_b", "k_b", "v_b")]
            + [spread_row(L0["scale"])]
            + [spread_row(L0[k]) for k in ("ln1_g", "ln1_b", "ln2_g", "ln2_b")] + [o_rows], axis=1),
        "w1_qkv": np.concatenate([L0[k].reshape(C, C) for k in ("q1", "k1", "v1")], axis=1),
        "w3_qkv": np.stack([taps(L0[k]) for k in ("q3", "k3", "v3")], axis=2)
                    .transpose(1, 0, 2, 3, 4).reshape(C, 3, 3, 3 * C),
        "w1_gi": np.concatenate([L0[k].reshape(EC, C) for k in ("g1", "i1")], axis=1),
        "w3_gi": np.stack([taps(L0[k]) for k in ("g3", "i3")], axis=2)
                   .transpose(1, 0, 2, 3, 4).reshape(EC, 3, 2, 3 * EC),
        "conv_w": np.stack([taps(L1[k]).reshape(3 * C, 3, C) for k in ("conv1_w", "conv2_w", "mask_w")], axis=1),
        "l1_qkv": np.stack([L1[k].reshape(C, C).T for k in ("q_w", "k_w", "v_w")], axis=1),
        "r1_t": L0["r1"].reshape(C, EC).T,
    }
    nc = bacc.Bacc("TRN2", target_bir_lowering=False, num_devices=1)
    feed, args = {}, []
    for name, v in arrays.items():
        v = np.ascontiguousarray(v)
        feed[f"in_{name}"] = v
        args.append(nc.dram_tensor(f"in_{name}", v.shape, mybir.dt.from_np(v.dtype), kind="ExternalInput").ap())
    args.append(nc.dram_tensor("out_x", (B, C, H, W), F32, kind="ExternalOutput").ap())
    build(nc, *args)
    return run_bass_kernel_spmd(nc, [feed], core_ids=[0]).results[0]["out_x"]
```

```python
from contextlib import ExitStack

import concourse.bass as bass
from concourse import mybir

F32 = mybir.dt.float32
BF16 = mybir.dt.bfloat16
ALU = mybir.AluOpType
ACT = mybir.ActivationFunctionType
AX = mybir.AxisListType

P = 128
B, C, H, W = 8, 32, 32, 32
PAIRS = B // 2
R = P // C
RH = H // R
BLK = RH * W
PW = W + 2
PLANE = (H + 2) * W
D = 4
EC = 64
EPS = 1e-5
SLOPE = 0.2
BANK = 512

TH, TW = 4, 8
KH, KW = TH + 2, TW + 2
KEYS = KH * KW
TA, TB = RH // TH, W // TW
UNITS = 2 * TA * TB
UPB = UNITS // 2
KSLOT = 64

GI_BANKS = (1, 3, 2, 0)

K_EQ, K_HEAD, K_SELJ, K_AVG, K_ID, K_WIN = 0, 32, 160, 164, 292, 420
K_END = K_WIN + UPB * KEYS
V_BC1, V_BC2, V_BM, V_BQ, V_BK, V_BV, V_SCALE, V_LN, V_OW = 0, 1, 2, 3, 4, 5, 6, 7, 7 + 4 * W
V_END = V_OW + D * C
I_MEAN, I_SHIFT, I_MOMENT, I_WAIT, I_BLOCK_VAR, I_VAR, I_RSTD = range(7)


class Signal:

    def __init__(self, sem, per_pair, start):
        self.sem, self.per_pair, self.start = sem, per_pair, start

    def at(self, pair, k):
        assert k or self.start, self.sem
        return pair * self.per_pair + (k + self.start)

    def before(self, pair):
        return self.at(pair, 0)

    def done(self, pair):
        return self.at(pair, self.per_pair)


def build(nc, x, shape_consts, vectors, w1_qkv, w3_qkv, w1_gi, w3_gi, conv_w, l1_qkv, r1_t, out):
    with ExitStack() as ctx:
        def sb(name, shape, dt=F32):
            return ctx.enter_context(nc.sbuf_tensor(name, shape, dt))

        def sem(name):
            return ctx.enter_context(nc.semaphore(name))

        signals = []

        def signal(name, per_pair, start=0):
            signals.append(Signal(sem(name), per_pair, start))
            return signals[-1]

        ps = ctx.enter_context(nc.psum_tensor("ps", [P, 8, BANK], F32))

        kc = sb("kc", [P, K_END])
        vec = sb("vec", [P, V_END])
        w1a = sb("w1a", [C, 3 * C])
        w3a = sb("w3a", [C, 3, 3, 3 * C])
        w1b = sb("w1b", [EC, 2 * C])
        w3b = sb("w3b", [EC, 3, 2, 3 * EC])
        w_conv = sb("w_conv", [P, 3, 3, C])
        w_qk = sb("w_qk", [P, 3, 2, 2, C])
        w_v = sb("w_v", [P, 3, C])
        w_gi = sb("w_gi", [3 * C, 3, 2, EC])
        w_bd = sb("w_bd", [P, 3, P])
        w_r1 = sb("w_r1", [P, 2, C])
        ident_bf = sb("ident_bf", [P, P], BF16)
        win_bf = sb("win_bf", [P, UPB * KEYS], BF16)
        inv_scale = sb("inv_scale", [P, 1])
        half_bm = sb("half_bm", [P, 1])
        ones = sb("ones", [P, 2 * BLK])
        neg_half = sb("neg_half", [P, 2 * RH])

        x_norm = sb("x_norm", [P, 2, BLK])
        x_res = sb("x_res", [P, 2, BLK])
        x1 = sb("x1", [P, 2, BLK])
        x2 = sb("x2", [P, 2, BLK])
        out_s = sb("out_s", [P, 2, BLK])
        ln1_out = sb("ln1_out", [P, 2, BLK])
        ln2_out = sb("ln2_out", [P, 2, BLK])
        act_c = sb("act_c", [P, 2, BLK])
        act_in = sb("act_in", [P, 2, BLK])
        w_in = sb("w_in", [P, 2, 2, 3, C])
        sh_ln1 = sb("sh_ln1", [P, 2, PLANE])
        sh_ln2 = sb("sh_ln2", [3 * C, 2, PLANE])
        sh_x2 = sb("sh_x2", [P, 2, PLANE])
        sh_in = sb("sh_in", [P, 2, PLANE])
        ln_c, ln_d, ln_q = [[sb(f"{t}_{n}", [P, 2 * RH, W]) for n in (1, 2)] for t in ("ln_c", "ln_d", "ln_q")]
        ln_s = [sb(f"ln_s_{n}", [P, 4, 2 * RH]) for n in (1, 2)]
        qk_t = sb("qk_t", [P, 2, BANK])
        v4 = sb("v4", [P, 2, BLK])
        sc_m = sb("sc_m", [P, 2 * D, C])
        sc_d = sb("sc_d", [P, 2 * D])
        sm = sb("sm", [P, 4, 2 * D])
        mix_p = sb("mix_p", [P, 2, D, C])
        mix_s = sb("mix_s", [P, 2, C])
        mix = sb("mix", [P, 2, R, C])
        gate = sb("gate", [P, 4, BANK])
        gi = sb("gi", [P, 2, BANK])
        hn = sb("hn", [P, 2, BLK])
        hc = sb("hc", [P, 2, BLK])
        st6 = sb("st6", [P, 2, 6])
        st = sb("st", [P, 2, 2])
        inorm_v = sb("inorm_v", [P, 7, 2])
        th = sb("th", [P, 2 * BLK])
        msk = sb("msk", [P, 2 * BLK])
        omm = sb("omm", [P, 2 * BLK])
        xm = sb("xm", [P, 2, RH + 2, PW])
        q_bd = sb("q_bd", [P, UNITS, R, TH * TW])
        k_h = sb("k_h", [P, 2, RH + 2, PW])
        xw = sb("xw", [P, UNITS, KEYS])
        v_t = sb("v_t", [P, UNITS // 2, P])
        prob = sb("prob", [P, UNITS, KSLOT])
        wsm = sb("wsm", [P, 3, UNITS])
        p_t = sb("p_t", [P, UNITS // 2 * R, 2, TH * TW])
        out1 = sb("out1", [P, 2 * BLK])
        res = sb("res", [P, 2 * BLK])
        pv = sb("pv", [P, 2 * BLK])
        dif = sb("dif", [P, 2 * BLK])
        table_in = sb("table_in", [P, 1])

        s_consts, s_vec = sem("shape_consts_loaded"), sem("vectors_loaded")
        s_w, s_diag = sem("fold_weights_loaded"), sem("other_weights_loaded")
        s_zero, s_zero_bd, s_late = sem("planes_cleared"), sem("weights_cleared"), sem("window_buffers_cleared")
        s_fold, s_wready = sem("folds_in_psum"), sem("constants_prepared")

        g_xn = signal("x_for_norm_loaded", 16)
        g_x = signal("x_for_sum_loaded", 16)
        g_ln = [signal("ln1_steps", 7), signal("ln2_steps", 7)]
        g_sq = [signal("ln1_squares", 1), signal("ln2_squares", 1)]
        g_rs = [signal("ln1_rstd", 1), signal("ln2_rstd", 1)]
        planes_by = {n: {e: signal(f"{n}_planes_{e}", 16 * R // 2 if e == "dma" else 1, start=1)
                         for e in (("dma",) if n == "ln1" else ()) + ("dve", "act")}
                     for n in ("ln1", "ln2", "x2", "in")}
        g_qkt = signal("qkt_in_psum", 2)
        g_qkt_sb = signal("qkt_in_sbuf", 2)
        g_v4 = signal("v4_in_psum", 1, start=1)
        g_v4_sb = signal("v4_in_sbuf", 1)
        g_gram = signal("gram_in_psum", 1, start=1)
        g_score = signal("score_steps", 11)
        g_rep = signal("scores_by_head", 1)
        g_pexp = signal("head_exp", 1)
        g_y = signal("attn_out_in_psum", 1, start=1)
        g_x1 = signal("x1_done", 1)
        g_i = signal("gate_info_in_psum", 4, start=1)
        g_gelu = signal("gelu_done", 4)
        g_gi = signal("gated", 4, start=1)
        g_r1 = signal("r1_in_psum", 1, start=1)
        g_x2 = signal("x2_done", 1, start=1)
        g_xw = signal("key_windows", 2 * TA)
        g_c1 = signal("conv1_in_psum", 1, start=1)
        g_c1_sb = signal("conv1_in_sbuf", 1)
        g_in = signal("inorm_steps", 7)
        g_avg = signal("inorm_averages", 2, start=1)
        g_inr = signal("inorm_rstd", 1)
        g_act = signal("conv1_centered", 1, start=1)
        g_win = signal("weights_scaled", 2)
        g_sc = signal("act_scaled", 1)
        g_lr = signal("lrelu_done", 1, start=1)
        g_mk = signal("mask_in_psum", 1)
        g_c2 = signal("conv2_in_psum", 1, start=1)
        g_th = signal("tanh_done", 1)
        g_xm = signal("masked_steps", 2, start=1)
        g_halo = signal("halo_copied", 1)
        g_q = signal("q_in_psum", 1)
        g_k = signal("k_in_psum", 1)
        g_v = signal("v_in_psum", 1, start=1)
        g_q_sb = signal("q_in_sbuf", 4)
        g_k_sb = signal("k_in_sbuf", 2)
        g_v_sb = signal("v_in_sbuf", 2)
        g_s = signal("sims_in_psum", 2, start=1)
        g_sm = signal("window_softmax_steps", 10)
        g_we = signal("window_exp", 2)
        g_t = signal("probs_t_in_psum", 2, start=1)
        g_t_sb = signal("probs_t_in_sbuf", 4, start=1)
        g_pv_sb = signal("window_out_in_sbuf", 1, start=1)
        g_pv = signal("window_out_in_psum", 1, start=1)
        g_o1 = signal("out1_in_sbuf", 1)
        g_res = signal("residual_steps", 4, start=1)
        g_fin = signal("final_steps", 2, start=1)
        g_out = signal("out_stored", 16, start=1)

        block = ctx.enter_context(nc.Block())

        x_dram, out_dram = [t.rearrange("n p m -> p n m") for t in (x, out)]

        def alone(engine):
            engine.wait_ge(s_zero, Z_PADS)

        def is_first(pair):
            return isinstance(pair, int) and pair == 0

        def conv1_bank(early):
            return 0 if early else 4

        def average_bank(early):
            return 2 if early else 5

        def mask_bank(early):
            return 3 if early else 6

        def conv2_bank(early):
            return 1 if early else 7

        def flat(t):
            return t.rearrange("p i m -> p (i m)")

        def plane(t):
            return t[:, :, :].rearrange("p i (y x) -> p i y x", x=W)

        def shift_copies(copy, src, planes, s, row_blocks):
            cut_left, cut_right = max(1 - s, 0), max(s - 1, 0)
            n = W - cut_left - cut_right
            for r in row_blocks:
                ins = copy(plane(planes)[C * s:C * s + C, :, 1 + RH * r:1 + RH * r + RH, cut_left:cut_left + n],
                           src[C * r:C * r + C, :, :].rearrange("p i (y x) -> p i y x", x=W)
                           [:, :, :, cut_right:cut_right + n])
            return ins

        Z_LN1, Z_PADS = 3, 7
        W_QKV, W_ALL = 3, 8


        @block.sync
        def _(sp):
            def load(dst, loaded, pair):
                sp.dma_start(flat(dst[:, :, :]).unsqueeze(1), x_dram[:, bass.ts(pair, 1), :])\
                  .then_inc(loaded.sem, 16)

            load(x_norm, g_xn, 0)
            sp.dma_start(vec[:, :], vectors).then_inc(s_vec, 16)
            sp.dma_start(w1b[:, :], w1_gi).then_inc(s_w, 16)
            sp.dma_start(w3b[:, :, :, :], w3_gi).then_inc(s_w, 16)
            sp.wait_ge(s_zero_bd, 3)
            sp.dma_start(w_conv[0:3 * C, :, :, :], conv_w).then_inc(s_diag, 16)
            for r in range(R):
                sp.dma_start(w_bd[C * r:C * r + C, :, C * r:C * r + C], l1_qkv).then_inc(s_diag, 16)
            for h in range(2):
                sp.dma_start(w_r1[EC * h:EC * h + EC, h, :], r1_t).then_inc(s_diag, 16)
            for g in signals:
                if g.start:
                    sp.sem_inc(g.sem, g.start)

            def ln1_planes(pair):
                sp.wait_ge(g_v4.sem, g_v4.before(pair))
                sp.wait_ge(g_ln[0].sem, g_ln[0].done(pair))
                for r in range(R // 2):
                    start = (1 + RH * r) * W
                    sp.dma_start(sh_ln1[C:2 * C, :, start:start + BLK], ln1_out[C * r:C * r + C])\
                      .then_inc(planes_by["ln1"]["dma"].sem, 16)

            def store(pair):
                alone(sp)
                sp.wait_ge(g_fin.sem, g_fin.done(pair))
                sp.dma_start(out_dram[:, bass.ts(pair, 1), :], flat(out_s[:, :, :]).unsqueeze(1))\
                  .then_inc(g_out.sem, 16)

            def load_norm(pair):
                if not isinstance(pair, int):
                    alone(sp)
                sp.wait_ge(g_ln[0].sem, g_ln[0].at(pair - 1, 2))
                load(x_norm, g_xn, pair)

            def load_res(pair):
                if not is_first(pair):
                    alone(sp)
                    sp.wait_ge(g_x1.sem, g_x1.done(pair - 1))
                load(x_res, g_x, pair)

            def step(pair, norm):
                if norm:
                    load_norm(pair + 3)
                load_res(pair + 2)
                if norm:
                    ln1_planes(pair + 3)
                store(pair)

            load_norm(1)
            sp.wait_ge(s_zero, Z_LN1)
            ln1_planes(0)
            load_res(0)
            ln1_planes(1)
            load_norm(2)
            load_res(1)
            ln1_planes(2)
            with sp.Fori(0, PAIRS - 3) as pair:
                step(pair, True)
            step(PAIRS - 3, False)
            but_last, last = PAIRS - 2, PAIRS - 1
            store(but_last)
            store(last)
            sp.wait_ge(g_out.sem, g_out.done(last))

        @block.gpsimd
        def _(pool):
            nc.gpsimd.memset(neg_half[:, :], -0.5).then_inc(s_zero, 1)
            nc.gpsimd.memset(ones[:, :], 1.0).then_inc(s_zero, 1)

            def clear(t, done=s_zero):
                nc.gpsimd.memset(t[:], 0.0).then_inc(done, 1)

            def rstd(n, pair):
                g, rs = g_ln[n], g_rs[n]
                pool.wait_ge(g.sem, g.at(pair, 5))
                nc.gpsimd.tensor_tensor(ln_s[n][:, 3, :], ln_s[n][:, 2, :], neg_half[:, :], ALU.pow)\
                  .then_inc(rs.sem, 1)

            def inorm_rstd(pair):
                pool.wait_ge(g_in.sem, g_in.at(pair, 7))
                nc.gpsimd.tensor_tensor(inorm_v[:, I_RSTD, :], inorm_v[:, I_VAR, :], neg_half[:, 0:2], ALU.pow)\
                  .then_inc(g_inr.sem, 1)

            def scaled_weights(pair):
                pool.wait_ge(g_inr.sem, g_inr.done(pair))
                pool.wait_ge(g_c2.sem, g_c2.before(pair))
                for i in range(2):
                    by_channel = inorm_v[:, I_RSTD, i:i + 1].broadcast_to([P, 2 * 3 * C])
                    nc.gpsimd.tensor_tensor(w_in[:, i, :, :, :].rearrange("p k y o -> p (k y o)"),
                                            w_conv[:, 1:3, :, :].rearrange("p k y o -> p (k y o)"),
                                            by_channel, ALU.mult).then_inc(g_win.sem, 1)

            def residual(pair):
                g = g_res
                pool.wait_ge(g_xm.sem, g_xm.at(pair, 1))
                pool.wait_ge(g_fin.sem, g_fin.before(pair))
                nc.gpsimd.tensor_tensor(omm[:, :], ones[:, :], msk[:, :], ALU.subtract).then_inc(g.sem, 1)
                pool.wait_ge(g_o1.sem, g_o1.done(pair))
                pool.wait_ge(g_x2.sem, g_x2.done(pair))
                nc.gpsimd.tensor_tensor(res[:, :], out1[:, :], flat(x2[:, :, :]), ALU.add).then_inc(g.sem, 1)
                pool.wait_ge(g.sem, g.at(pair, 1))
                nc.gpsimd.tensor_tensor(dif[:, :], omm[:, :], out1[:, :], ALU.mult).then_inc(g.sem, 1)
                pool.wait_ge(g.sem, g.at(pair, 3))
                nc.gpsimd.tensor_tensor(res[:, :], res[:, :], dif[:, :], ALU.subtract).then_inc(g.sem, 1)

            def final(pair):
                g = g_fin
                pool.wait_ge(g_pv_sb.sem, g_pv_sb.done(pair))
                nc.gpsimd.tensor_tensor(dif[:, :], pv[:, :], omm[:, :], ALU.mult).then_inc(g.sem, 1)
                pool.wait_ge(g.sem, g.at(pair, 1))
                pool.wait_ge(g_out.sem, g_out.before(pair))
                nc.gpsimd.tensor_tensor(flat(out_s[:, :, :]), dif[:, :], res[:, :], ALU.add).then_inc(g.sem, 1)

            def step(pair, norm):
                residual(pair)
                if norm:
                    rstd(0, pair + 3)
                rstd(1, pair + 2)
                inorm_rstd(pair + 1)
                scaled_weights(pair + 1)
                final(pair)

            clear(sh_ln1)
            pool.wait_ge(s_zero, 1)
            rstd(0, 0)
            clear(sh_ln2)
            clear(sh_x2)
            clear(sh_in)
            rstd(0, 1)
            clear(xm)
            clear(q_bd, s_late)
            clear(prob, s_late)
            clear(p_t, s_late)
            rstd(1, 0)
            rstd(0, 2)
            pool.wait_ge(s_diag, 16 * (1 + R + 2))
            rstd(1, 1)
            inorm_rstd(0)
            scaled_weights(0)
            with pool.Fori(0, PAIRS - 3) as pair:
                step(pair, True)
            step(PAIRS - 3, False)
            but_last, last = PAIRS - 2, PAIRS - 1
            residual(but_last)
            inorm_rstd(last)
            scaled_weights(last)
            final(but_last)
            residual(last)

        @block.scalar
        def _(act):
            act.dma_start(w1a[:, :], w1_qkv).then_inc(s_w, 16)
            act.dma_start(w3a[:, :, :, :], w3_qkv).then_inc(s_w, 16)
            act.dma_start(kc[:, :], shape_consts).then_inc(s_consts, 16)

            def squares(n, pair):
                g, sq = g_ln[n], g_sq[n]
                act.wait_ge(g.sem, g.at(pair, 2))
                nc.scalar.activation(ln_q[n][:, :, :], ln_c[n][:, :, :], ACT.Square).then_inc(sq.sem, 1)

            def act_copy(o, i):
                return nc.scalar.activation(o, i, ACT.Copy)

            def planes(name, src, dst, src_ready, reader, pair):
                act.wait_ge(src_ready.sem, src_ready.done(pair))
                act.wait_ge(reader.sem, reader.before(pair))
                shift_copies(act_copy, src, dst, 1, range(R // 2, R) if name == "ln1" else (R - 1,))
                shift_copies(act_copy, src, dst, 2, range(R)).then_inc(planes_by[name]["act"].sem, 1)

            def qk_t_evac(pair, i):
                act.wait_ge(g_qkt.sem, g_qkt.at(pair, i + 1))
                act.wait_ge(g_gram.sem, g_gram.before(pair))
                nc.scalar.activation(qk_t[:, i, :], ps[:, i, :], ACT.Copy).then_inc(g_qkt_sb.sem, 1)

            def v4_evac(pair):
                act.wait_ge(g_v4.sem, g_v4.done(pair))
                act.wait_ge(g_y.sem, g_y.before(pair))
                nc.scalar.activation(v4[:, :, :].rearrange("p i m -> p (i m)"), ps[:, 2, :], ACT.Copy)\
                  .then_inc(g_v4_sb.sem, 1)

            def load_exp_table():
                nc.scalar.activation(table_in[:, :], vec[:, V_SCALE:V_SCALE + 1], ACT.Exp)

            def head_exp(pair):
                act.wait_ge(g_score.sem, g_score.at(pair, 5))
                nc.scalar.activation(sm[:, 2, :], sm[:, 1, :], ACT.Exp).then_inc(g_pexp.sem, 1)

            def gelu(pair, n):
                act.wait_ge(g_i.sem, g_i.at(pair, n + 1))
                act.wait_ge(g_gi.sem, g_gi.before(pair))
                nc.scalar.activation(gate[EC:P, n, :], ps[0:EC, GI_BANKS[n], :], ACT.Gelu).then_inc(g_gelu.sem, 1)

            def conv1_evac(pair, early=False):
                act.wait_ge(g_in.sem, g_in.at(pair, 1))
                act.wait_ge(g_act.sem, g_act.before(pair))
                nc.scalar.activation(hc[:, :, :].rearrange("p i m -> p (i m)"), ps[:, conv1_bank(early), :],
                                     ACT.Identity, bias=vec[:, V_BC1:V_BC1 + 1]).then_inc(g_c1_sb.sem, 1)

            def tanh_mask(pair, early=False):
                act.wait_ge(g_mk.sem, g_mk.done(pair))
                act.wait_ge(g_xm.sem, g_xm.before(pair))
                act.wait_ge(g_res.sem, g_res.before(pair))
                nc.scalar.activation(th[:, :], ps[:, mask_bank(early), :], ACT.Tanh, bias=half_bm[:, 0:1],
                                     scale=0.5)\
                  .then_inc(g_th.sem, 1)

            def out1_evac(pair, early=False):
                act.wait_ge(g_c2.sem, g_c2.done(pair))
                act.wait_ge(g_res.sem, g_res.before(pair))
                nc.scalar.activation(out1[:, :], ps[:, conv2_bank(early), :], ACT.Identity,
                                     bias=vec[:, V_BC2:V_BC2 + 1])\
                  .then_inc(g_o1.sem, 1)

            def q_evac(pair):
                act.wait_ge(g_q.sem, g_q.done(pair))
                act.wait_ge(g_s.sem, g_s.before(pair))
                for r in range(R // 2):
                    rows = slice(C * r, C * r + C)
                    nc.scalar.activation(q_bd[rows, :, r, :],
                                         ps[rows, 4, :].rearrange("p (u m) -> p u m", u=UNITS), ACT.Identity,
                                         bias=vec[rows, V_BQ:V_BQ + 1]).then_inc(g_q_sb.sem, 1)

            def k_evac(pair):
                act.wait_ge(g_k.sem, g_k.done(pair))
                for i in range(2):
                    nc.scalar.activation(k_h[:, i, :, :].rearrange("p y x -> p (y x)"),
                                         ps[:, 5 + i, 0:(RH + 2) * PW], ACT.Identity,
                                         bias=vec[:, V_BK:V_BK + 1]).then_inc(g_k_sb.sem, 1)

            def key_windows(pair):
                act.wait_ge(g_halo.sem, g_halo.done(pair))
                act.wait_ge(g_v.sem, g_v.before(pair))
                for ia in range(2 * TA):
                    i, a = ia // TA, ia % TA
                    for b in range(TB):
                        ins = nc.scalar.activation(
                            xw[:, TB * ia + b, :].rearrange("p (y x) -> p y x", x=KW),
                            xm[:, i, TH * a:TH * a + KH, TW * b:TW * b + KW], ACT.Copy)
                    ins.then_inc(g_xw.sem, 1)

            def window_exp(pair):
                for h in range(2):
                    act.wait_ge(g_sm.sem, g_sm.at(pair, 2 * h + 2))
                    pr = prob[:, UPB * h:UPB * h + UPB, 0:KEYS]
                    nc.scalar.activation(pr, pr, ACT.Exp).then_inc(g_we.sem, 1)

            def probs_t(pair):
                act.wait_ge(g_pv.sem, g_pv.before(pair))
                for t in range(2):
                    act.wait_ge(g_t.sem, g_t.at(pair, t + 1))
                    for h in range(2):
                        rows = slice(KSLOT * h, KSLOT * h + KSLOT)
                        nc.scalar.activation(p_t[rows, 4 * R * t:4 * R * t + 4 * R, h, :],
                                             ps[rows, (7, 4)[t], :].rearrange("p (q m) -> p q m", m=TH * TW),
                                             ACT.Copy).then_inc(g_t_sb.sem, 1)

            def pv_evac(pair):
                act.wait_ge(g_pv.sem, g_pv.done(pair))
                act.wait_ge(g_fin.sem, g_fin.before(pair))
                nc.scalar.activation(pv[:, :], ps[:, 5, :], ACT.Identity, bias=vec[:, V_BV:V_BV + 1])\
                  .then_inc(g_pv_sb.sem, 1)

            def ln1_planes(pair):
                planes("ln1", ln1_out, sh_ln1, g_ln[0], g_v4, pair)

            def ln2_planes(pair):
                planes("ln2", ln2_out, sh_ln2, g_ln[1], g_i, pair)

            def x2_planes(pair):
                planes("x2", x2, sh_x2, g_x2, g_c1, pair)

            def in_planes(pair):
                planes("in", act_c, sh_in, g_lr, g_c2, pair)

            def step(pair, norm):
                load_exp_table()
                squares(1, pair + 1)
                conv1_evac(pair)
                qk_t_evac(pair + 2, 0)
                qk_t_evac(pair + 2, 1)
                in_planes(pair)
                v4_evac(pair + 2)
                ln2_planes(pair + 1)
                tanh_mask(pair)
                head_exp(pair + 2)
                q_evac(pair)
                k_evac(pair)
                out1_evac(pair)
                key_windows(pair)
                if norm:
                    squares(0, pair + 3)
                window_exp(pair)
                gelu(pair + 1, 0)
                gelu(pair + 1, 1)
                if norm:
                    ln1_planes(pair + 3)
                gelu(pair + 1, 2)
                gelu(pair + 1, 3)
                probs_t(pair)
                x2_planes(pair + 1)
                pv_evac(pair)

            act.wait_ge(s_vec, 16)
            load_exp_table()
            squares(0, 0)
            act.wait_ge(s_zero, Z_LN1)
            ln1_planes(0)
            squares(0, 1)
            qk_t_evac(0, 0)
            qk_t_evac(0, 1)
            head_exp(0)
            v4_evac(0)
            ln1_planes(1)
            squares(1, 0)
            qk_t_evac(1, 0)
            qk_t_evac(1, 1)
            act.wait_ge(s_zero, Z_PADS)
            ln2_planes(0)
            v4_evac(1)
            head_exp(1)
            squares(0, 2)
            gelu(0, 0)
            gelu(0, 1)
            gelu(0, 2)
            gelu(0, 3)
            x2_planes(0)
            ln1_planes(2)
            act.wait_ge(s_wready, W_ALL)
            act.wait_ge(s_late, 5)
            with act.Fori(0, PAIRS - 3) as pair:
                step(pair, True)
            step(PAIRS - 3, False)
            but_last, last = PAIRS - 2, PAIRS - 1
            load_exp_table()
            squares(1, last)
            conv1_evac(but_last)
            in_planes(but_last)
            ln2_planes(last)
            tanh_mask(but_last)
            out1_evac(but_last)
            gelu(last, 0)
            gelu(last, 1)
            q_evac(but_last)
            k_evac(but_last)
            gelu(last, 2)
            gelu(last, 3)
            key_windows(but_last)
            x2_planes(last)
            window_exp(but_last)
            conv1_evac(last, True)
            in_planes(last)
            tanh_mask(last, True)
            probs_t(but_last)
            pv_evac(but_last)
            q_evac(last)
            k_evac(last)
            key_windows(last)
            window_exp(last)
            out1_evac(last, True)
            probs_t(last)

        @block.vector
        def _(dve):
            for t in (w_bd, w_r1, w_conv, ps[:, 0, 0:12 * C], ps[:, 2, 0:3 * C]):
                nc.vector.memset(t[:], 0.0).then_inc(s_zero_bd, 1)
            dve.wait_ge(s_vec, 16)

            def folded_qkv():
                dve.wait_ge(s_fold, 1)
                qk_f = ps[:, 0, 0:12 * C].rearrange("p (d m y o) -> p d m y o", d=2, m=2, o=C)
                for d in range(2):
                    nc.vector.tensor_copy(w_qk[:, :, d, :, :].rearrange("p y m o -> p m y o"), qk_f[:, d])\
                      .then_inc(s_wready, 1)
                nc.vector.tensor_copy(w_v[:, :, :], ps[:, 2, 0:3 * C].rearrange("p (y o) -> p y o", o=C))\
                  .then_inc(s_wready, 1)

            def other_constants():
                dve.wait_ge(s_fold, 2)
                gi_f = ps[0:3 * C, 1, 0:6 * EC].rearrange("p (m y o) -> p m y o", m=2, o=EC)
                nc.vector.tensor_copy(w_gi[:, :, :, :].rearrange("p y m o -> p m y o"), gi_f)\
                  .then_inc(s_wready, 1)
                nc.vector.reciprocal(inv_scale[:, :], vec[:, V_SCALE:V_SCALE + 1]).then_inc(s_wready, 1)
                nc.vector.tensor_scalar(half_bm[:, :], vec[:, V_BM:V_BM + 1], 0.5, None, ALU.mult)\
                  .then_inc(s_wready, 1)
                dve.wait_ge(s_consts, 16)
                nc.vector.tensor_copy(ident_bf[:, :], kc[:, K_ID:K_ID + P]).then_inc(s_wready, 1)
                nc.vector.tensor_copy(win_bf[:, :], kc[:, K_WIN:K_END]).then_inc(s_wready, 1)
                dve.wait_ge(s_wready, W_ALL)

            def clear(*buffers):
                for t in buffers:
                    nc.vector.memset(t[:], 0.0).then_inc(s_late, 1)

            def ln_per_row(n, k):
                return ln_s[n][:, k, :].unsqueeze(2).broadcast_to([P, 2 * RH, W])

            def ln_per_col(k):
                return vec[:, V_LN + W * k:V_LN + W * k + W].unsqueeze(1).broadcast_to([P, 2 * RH, W])

            def ln_center(n, src, pair):
                g = g_ln[n]
                x3 = src.rearrange("p i (y x) -> p (i y) x", x=W)
                nc.vector.reduce_sum(ln_s[n][:, 0, :], x3, AX.X).then_inc(g.sem, 1)
                dve.wait_ge(g.sem, g.at(pair, 1))
                nc.vector.scalar_tensor_tensor(out=ln_c[n][:, :, :], in0=ln_per_row(n, 0), scalar=1.0 / W, in1=x3,
                                               op0=ALU.mult, op1=ALU.subtract).then_inc(g.sem, 1)
                dve.wait_ge(g.sem, g.at(pair, 2))
                nc.vector.tensor_tensor(ln_d[n][:, :, :], ln_c[n][:, :, :], ln_per_col(2 * n), ALU.mult)\
                  .then_inc(g.sem, 1)

            def ln_var(n, pair):
                g, sq = g_ln[n], g_sq[n]
                dve.wait_ge(sq.sem, sq.done(pair))
                nc.vector.reduce_sum(ln_s[n][:, 1, :], ln_q[n][:, :, :], AX.X).then_inc(g.sem, 1)
                dve.wait_ge(g.sem, g.at(pair, 4))
                nc.vector.tensor_scalar(ln_s[n][:, 2, :], ln_s[n][:, 1, :], 1.0 / W, EPS, ALU.mult, ALU.add)\
                  .then_inc(g.sem, 1)

            def ln_apply(n, dst, name, pair):
                g, rs = g_ln[n], g_rs[n]
                dve.wait_ge(rs.sem, rs.done(pair))
                nc.vector.tensor_tensor(ln_d[n][:, :, :], ln_d[n][:, :, :], ln_per_row(n, 3), ALU.mult)\
                  .then_inc(g.sem, 1)
                dve.wait_ge(g.sem, g.at(pair, 6))
                planes_read(name, pair)
                nc.vector.tensor_tensor(dst[:, :, :].rearrange("p i (y x) -> p (i y) x", x=W),
                                        ln_per_col(2 * n + 1), ln_d[n][:, :, :], ALU.subtract).then_inc(g.sem, 1)

            def planes_read(name, pair):
                for engine, g in planes_by[name].items():
                    if engine != "dve":
                        dve.wait_ge(g.sem, g.before(pair))

            def planes(name, src, dst, src_ready, reader, pair):
                dve.wait_ge(src_ready.sem, src_ready.done(pair))
                dve.wait_ge(reader.sem, reader.before(pair))
                if name == "ln1":
                    shift_copies(nc.vector.tensor_copy, src, dst, 3, range(R))
                else:
                    shift_copies(nc.vector.tensor_copy, src, dst, 1, range(R - 1))
                shift_copies(nc.vector.tensor_copy, src, dst, 0, range(R)).then_inc(planes_by[name]["dve"].sem, 1)

            def ln1_center(pair):
                dve.wait_ge(g_xn.sem, g_xn.done(pair))
                ln_center(0, x_norm[:, :, :], pair)

            def ln1_apply(pair):
                ln_apply(0, ln1_out, "ln1", pair)
                planes("ln1", ln1_out, sh_ln1, g_ln[0], g_v4, pair)

            sm3 = [sm[:, k, :].rearrange("p (i e) -> p i e", e=D) for k in range(3)]

            def per_image(col):
                return sm[:, 3, col:col + 2].unsqueeze(2).broadcast_to([P, 2, D])

            def head_scores(pair):
                g = g_score
                dve.wait_ge(g_gram.sem, g_gram.done(pair))
                eq = kc[:, K_EQ:K_EQ + C].unsqueeze(1).broadcast_to([P, 2 * D, C])
                nc.vector.tensor_tensor(sc_m[:, :, :], ps[:, 3, 0:2 * P].rearrange("p (e c) -> p e c", c=C),
                                        eq, ALU.mult).then_inc(g.sem, 1)
                dve.wait_ge(g.sem, g.at(pair, 1))
                nc.vector.reduce_sum(sc_d[:, :], sc_m[:, :, :], AX.X).then_inc(g.sem, 1)

            def head_max(pair):
                g = g_score
                dve.wait_ge(g_rep.sem, g_rep.done(pair))
                nc.vector.tensor_scalar(sm[:, 0, :], ps[:, 3, 2 * P:2 * P + 2 * D], inv_scale[:, 0:1], None,
                                        ALU.mult).then_inc(g.sem, 1)
                dve.wait_ge(g.sem, g.at(pair, 3))
                nc.vector.reduce_max(sm[:, 3, 0:2], sm3[0], AX.X).then_inc(g.sem, 1)
                dve.wait_ge(g.sem, g.at(pair, 4))
                nc.vector.tensor_tensor(sm3[1], sm3[0], per_image(0), ALU.subtract).then_inc(g.sem, 1)

            def head_mix(pair):
                g = g_score
                dve.wait_ge(g_pexp.sem, g_pexp.done(pair))
                nc.vector.reduce_sum(sm[:, 3, 2:4], sm3[2], AX.X).then_inc(g.sem, 1)
                dve.wait_ge(g.sem, g.at(pair, 6))
                nc.vector.reciprocal(sm[:, 3, 4:6], sm[:, 3, 2:4]).then_inc(g.sem, 1)
                dve.wait_ge(g.sem, g.at(pair, 7))
                nc.vector.tensor_tensor(sm3[0], sm3[2], per_image(4), ALU.mult).then_inc(g.sem, 1)
                dve.wait_ge(g.sem, g.at(pair, 8))
                for i in range(2):
                    p_b = sm[:, 0, D * i:D * i + D].unsqueeze(2).broadcast_to([P, D, C])
                    ow = vec[:, V_OW:V_OW + D * C].rearrange("p (e o) -> p e o", o=C)
                    mul = nc.vector.tensor_tensor(mix_p[:, i, :, :], ow, p_b, ALU.mult)
                mul.then_inc(g.sem, 1)
                dve.wait_ge(g.sem, g.at(pair, 9))
                nc.vector.reduce_sum(mix_s[:, :, :], mix_p[:, :, :, :].rearrange("p i e o -> p i o e"), AX.X)\
                  .then_inc(g.sem, 1)
                dve.wait_ge(g.sem, g.at(pair, 10))
                sel = kc[:, K_SELJ:K_SELJ + R].unsqueeze(2).broadcast_to([P, R, C])
                for i in range(2):
                    mul = nc.vector.tensor_tensor(mix[:, i, :, :], sel,
                                                  mix_s[:, i, :].unsqueeze(1).broadcast_to([P, R, C]), ALU.mult)
                mul.then_inc(g.sem, 1)

            def ln2_center(pair):
                dve.wait_ge(g_y.sem, g_y.done(pair))
                dve.wait_ge(g_x.sem, g_x.done(pair))
                nc.vector.tensor_tensor(flat(x1[:, :, :]), ps[:, 3, :], flat(x_res[:, :, :]), ALU.add)\
                  .then_inc(g_x1.sem, 1)
                dve.wait_ge(g_x1.sem, g_x1.done(pair))
                ln_center(1, x1[:, :, :], pair)

            def ln2_apply(pair):
                ln_apply(1, ln2_out, "ln2", pair)
                planes("ln2", ln2_out, sh_ln2, g_ln[1], g_i, pair)

            def gated(pair, n):
                dve.wait_ge(g_gelu.sem, g_gelu.at(pair, n + 1))
                dve.wait_ge(g_r1.sem, g_r1.before(pair))
                nc.vector.tensor_tensor(gi[EC * (n % 2):EC * (n % 2) + EC, n // 2, :], ps[EC:P, GI_BANKS[n], :],
                                        gate[EC:P, n, :], ALU.mult).then_inc(g_gi.sem, 1)

            def x2_sum(pair):
                dve.wait_ge(g_r1.sem, g_r1.done(pair))
                dve.wait_ge(g_res.sem, g_res.before(pair))
                planes_read("x2", pair)
                nc.vector.tensor_tensor(flat(x2[:, :, :]), ps[:, 1, :], flat(x1[:, :, :]), ALU.add)\
                  .then_inc(g_x2.sem, 1)

            def inorm(pair, early=False):
                g = g_in
                dve.wait_ge(g_c1.sem, g_c1.done(pair))
                dve.wait_ge(g_avg.sem, g_avg.before(pair))
                for i in range(2):
                    ins = nc.vector.bn_stats(st6[:, i, :], ps[:, conv1_bank(early), BLK * i:BLK * i + BLK])
                ins.then_inc(g.sem, 1)
                dve.wait_ge(g.sem, g.at(pair, 1))
                nc.vector.memset(inorm_v[:, I_WAIT, :], 0.0)
                for i in range(2):
                    ins = nc.vector.bn_aggr(st[:, i, :], st6[:, i, :])
                ins.then_inc(g.sem, 1)
                dve.wait_ge(g.sem, g.at(pair, 2))
                nc.vector.tensor_scalar(inorm_v[:, I_BLOCK_VAR, :], st[:, :, 1], EPS, None, ALU.add)\
                  .then_inc(g.sem, 1)

            def inorm_mean(pair, early=False):
                g = g_in
                dve.wait_ge(g_avg.sem, g_avg.at(pair, 1))
                nc.vector.tensor_tensor(inorm_v[:, I_SHIFT, :], st[:, :, 0], ps[:, average_bank(early), 0:2],
                                        ALU.subtract)\
                  .then_inc(g.sem, 1)
                nc.vector.tensor_scalar(inorm_v[:, I_MEAN, :], ps[:, average_bank(early), 0:2],
                                        vec[:, V_BC1:V_BC1 + 1], None, ALU.add)\
                  .then_inc(g.sem, 1)
                dve.wait_ge(g.sem, g.at(pair, 4))
                for i in range(2):
                    shift = inorm_v[:, I_SHIFT, i:i + 1]
                    ins = nc.vector.scalar_tensor_tensor(
                        out=inorm_v[:, I_MOMENT, i:i + 1], in0=shift, scalar=shift,
                        in1=inorm_v[:, I_BLOCK_VAR, i:i + 1], op0=ALU.mult, op1=ALU.add)
                ins.then_inc(g.sem, 1)

            def center(pair):
                dve.wait_ge(g_c1_sb.sem, g_c1_sb.done(pair))
                dve.wait_ge(g_in.sem, g_in.at(pair, 5))
                dve.wait_ge(g_lr.sem, g_lr.before(pair))
                for i in range(2):
                    ins = nc.vector.tensor_scalar(hn[:, i, :], hc[:, i, :], inorm_v[:, I_MEAN, i:i + 1], None,
                                                  ALU.subtract)
                ins.then_inc(g_act.sem, 1)

            def variance(pair, early=False):
                dve.wait_ge(g_avg.sem, g_avg.at(pair, 2))
                nc.vector.tensor_copy(inorm_v[:, I_VAR, :], ps[:, average_bank(early), 2:4]).then_inc(g_in.sem, 1)

            def lrelu(pair):
                dve.wait_ge(g_c2.sem, g_c2.before(pair))
                dve.wait_ge(g_act.sem, g_act.done(pair))
                planes_read("in", pair)
                nc.vector.scalar_tensor_tensor(out=flat(act_c[:, :, :]), in0=flat(hn[:, :, :]), scalar=SLOPE,
                                               in1=flat(hn[:, :, :]), op0=ALU.mult, op1=ALU.max)\
                  .then_inc(g_lr.sem, 1)

            def in_planes(pair):
                planes("in", act_c, sh_in, g_lr, g_c2, pair)

            def scaled_act(pair):
                dve.wait_ge(g_inr.sem, g_inr.done(pair))
                dve.wait_ge(g_lr.sem, g_lr.done(pair))
                dve.wait_ge(g_xm.sem, g_xm.before(pair))
                for i in range(2):
                    ins = nc.vector.tensor_scalar(act_in[:, i, :], act_c[:, i, :], inorm_v[:, I_RSTD, i:i + 1],
                                                  None, ALU.mult)
                ins.then_inc(g_sc.sem, 1)

            def masked(pair):
                dve.wait_ge(g_th.sem, g_th.done(pair))
                nc.vector.tensor_scalar(msk[:, :], th[:, :], 0.5, 0.5, ALU.mult, ALU.add).then_inc(g_xm.sem, 1)
                dve.wait_ge(g_xm.sem, g_xm.at(pair, 1))
                dve.wait_ge(g_sc.sem, g_sc.done(pair))
                dve.wait_ge(g_v.sem, g_v.before(pair))
                nc.vector.tensor_tensor(xm[:, :, 1:1 + RH, 1:1 + W],
                                        msk[:, :].rearrange("p (i y x) -> p i y x", i=2, x=W),
                                        act_in[:, :, :].rearrange("p i (y x) -> p i y x", x=W), ALU.mult)\
                  .then_inc(g_xm.sem, 1)
                dve.wait_ge(g_xm.sem, g_xm.at(pair, 2))
                for r in range(R - 1):
                    nc.vector.tensor_copy(xm[C * r + C:C * r + 2 * C, :, 0, :], xm[C * r:C * r + C, :, RH, :])
                    ins = nc.vector.tensor_copy(xm[C * r:C * r + C, :, RH + 1, :],
                                                xm[C * r + C:C * r + 2 * C, :, 1, :])
                ins.then_inc(g_halo.sem, 1)

            def q_evac(pair):
                dve.wait_ge(g_q.sem, g_q.done(pair))
                dve.wait_ge(g_s.sem, g_s.before(pair))
                for r in range(R // 2, R):
                    rows = slice(C * r, C * r + C)
                    nc.vector.tensor_scalar(q_bd[rows, :, r, :],
                                            ps[rows, 4, :].rearrange("p (u m) -> p u m", u=UNITS),
                                            vec[rows, V_BQ:V_BQ + 1], None, ALU.add).then_inc(g_q_sb.sem, 1)

            def v_evac(pair):
                dve.wait_ge(g_v.sem, g_v.done(pair))
                dve.wait_ge(g_pv.sem, g_pv.before(pair))
                for h in range(2):
                    nc.vector.tensor_copy(v_t[:, 4 * h:4 * h + 4, :].rearrange("p u m -> p (u m)"),
                                          ps[:, (7, 4)[h], :]).then_inc(g_v_sb.sem, 1)

            def window_softmax(pair):
                g = g_sm
                dve.wait_ge(g_t.sem, g_t.before(pair))
                for h in range(2):
                    units = slice(UPB * h, UPB * h + UPB)
                    sims = ps[:, 5 + h, 0:UPB * KEYS].rearrange("p (u k) -> p u k", k=KEYS)
                    dve.wait_ge(g_s.sem, g_s.at(pair, h + 1))
                    nc.vector.reduce_max(wsm[:, 0, units], sims, AX.X).then_inc(g.sem, 1)
                    dve.wait_ge(g.sem, g.at(pair, 2 * h + 1))
                    nc.vector.tensor_tensor(prob[:, units, 0:KEYS], sims, wsm[:, 0, units].unsqueeze(2)
                                            .broadcast_to([P, UPB, KEYS]), ALU.subtract).then_inc(g.sem, 1)

            def window_probs(pair):
                g = g_sm
                for h in range(2):
                    units = slice(UPB * h, UPB * h + UPB)
                    dve.wait_ge(g_we.sem, g_we.at(pair, h + 1))
                    nc.vector.reduce_sum(wsm[:, 1, units], prob[:, units, 0:KEYS], AX.X).then_inc(g.sem, 1)
                    dve.wait_ge(g.sem, g.at(pair, 3 * h + 5))
                    nc.vector.reciprocal(wsm[:, 2, units], wsm[:, 1, units]).then_inc(g.sem, 1)
                    dve.wait_ge(g.sem, g.at(pair, 3 * h + 6))
                    nc.vector.tensor_tensor(prob[:, units, 0:KEYS], prob[:, units, 0:KEYS], wsm[:, 2, units]
                                            .unsqueeze(2).broadcast_to([P, UPB, KEYS]), ALU.mult)\
                      .then_inc(g.sem, 1)

            def final(pair):
                g = g_fin
                dve.wait_ge(g_fin.sem, g_fin.before(pair))
                dve.wait_ge(g_res.sem, g_res.done(pair))
                dve.wait_ge(g_pv.sem, g_pv.done(pair))
                nc.vector.scalar_tensor_tensor(out=dif[:, :], in0=ps[:, 5, :], scalar=vec[:, V_BV:V_BV + 1],
                                               in1=omm[:, :], op0=ALU.add, op1=ALU.mult).then_inc(g.sem, 1)
                dve.wait_ge(g.sem, g.at(pair, 1))
                dve.wait_ge(g_out.sem, g_out.before(pair))
                nc.vector.tensor_tensor(flat(out_s[:, :, :]), dif[:, :], res[:, :], ALU.add).then_inc(g.sem, 1)

            def x2_all(pair):
                x2_sum(pair)
                planes("x2", x2, sh_x2, g_x2, g_c1, pair)

            def step(pair, norm):
                ln2_center(pair + 1)
                ln_var(1, pair + 1)
                inorm(pair)
                inorm_mean(pair)
                center(pair)
                variance(pair)
                lrelu(pair)
                in_planes(pair)
                head_scores(pair + 2)
                ln2_apply(pair + 1)
                scaled_act(pair)
                head_max(pair + 2)
                masked(pair)
                head_mix(pair + 2)
                q_evac(pair)
                if norm:
                    ln1_center(pair + 3)
                window_softmax(pair)
                if norm:
                    ln_var(0, pair + 3)
                v_evac(pair)
                window_probs(pair)
                if norm:
                    ln1_apply(pair + 3)
                gated(pair + 1, 0)
                gated(pair + 1, 1)
                gated(pair + 1, 2)
                gated(pair + 1, 3)
                x2_all(pair + 1)

            ln1_center(0)
            ln_var(0, 0)
            folded_qkv()
            dve.wait_ge(s_zero, Z_LN1)
            ln1_apply(0)
            ln1_center(1)
            ln_var(0, 1)
            other_constants()
            clear(ps[:, 4, :], ps[:, 7, :])
            ln_apply(0, ln1_out, "ln1", 1)
            head_scores(0)
            head_max(0)
            head_mix(0)
            planes("ln1", ln1_out, sh_ln1, g_ln[0], g_v4, 1)
            ln2_center(0)
            ln_var(1, 0)
            dve.wait_ge(s_zero, Z_PADS)
            ln2_apply(0)
            head_scores(1)
            head_max(1)
            ln1_center(2)
            head_mix(1)
            ln_var(0, 2)
            dve.wait_ge(s_late, 5)
            gated(0, 0)
            gated(0, 1)
            gated(0, 2)
            gated(0, 3)
            x2_all(0)
            ln1_apply(2)
            with dve.Fori(0, PAIRS - 3) as pair:
                step(pair, True)
            step(PAIRS - 3, False)
            but_last, last = PAIRS - 2, PAIRS - 1
            ln2_center(last)
            ln_var(1, last)
            inorm(but_last)
            inorm_mean(but_last)
            center(but_last)
            variance(but_last)
            lrelu(but_last)
            in_planes(but_last)
            ln2_apply(last)
            scaled_act(but_last)
            masked(but_last)
            gated(last, 0)
            gated(last, 1)
            q_evac(but_last)
            gated(last, 2)
            gated(last, 3)
            x2_all(last)
            window_softmax(but_last)
            inorm(last, True)
            inorm_mean(last, True)
            center(last)
            variance(last, True)
            lrelu(last)
            in_planes(last)
            v_evac(but_last)
            window_probs(but_last)
            scaled_act(last)
            masked(last)
            q_evac(last)
            window_softmax(last)
            window_probs(last)
            v_evac(last)
            final(last)

        @block.tensor
        def _(pe):
            pe.wait_ge(s_w, 64)
            pe.wait_ge(s_zero_bd, 5)
            for d in range(2):
                for m in range(2):
                    for s in range(3):
                        at, q = 3 * C * (2 * d + m), C * (s + d)
                        nc.tensor.matmul(ps[q:q + C, 0, at:at + 3 * C], w1a[:, C * m:C * m + C],
                                         w3a[:, s, m, :], start=True, stop=True)
            for s in range(3):
                mm = nc.tensor.matmul(ps[C * s:C * s + C, 2, 0:3 * C], w1a[:, 2 * C:3 * C], w3a[:, s, 2, :],
                                      start=True, stop=True)
            mm.then_inc(s_fold, 1)
            for m in range(2):
                for s in range(3):
                    mm = nc.tensor.matmul(ps[C * s:C * s + C, 1, 3 * EC * m:3 * EC * m + 3 * EC],
                                          w1b[:, C * m:C * m + C], w3b[:, s, m, :], start=True, stop=True)
            mm.then_inc(s_fold, 1)

            def block_conv(planes, bank, weight):
                for dy in range(3):
                    for r in range(R):
                        mm = nc.tensor.matmul(ps[C * r:C * r + C, bank, :], weight(dy),
                                              plane(planes)[:, :, RH * r + dy:RH * r + dy + RH, 0:W],
                                              start=(dy == 0), stop=(dy == 2))
                return mm

            def planes_ready(name, pair):
                for g in planes_by[name].values():
                    pe.wait_ge(g.sem, g.done(pair))

            def qk(pair, i, halves=(0, 1)):
                planes_ready("ln1", pair)
                if i == 1 and not is_first(pair):
                    pe.wait_ge(g_x2.sem, g_x2.before(pair - 1))
                for h in halves:
                    for d in range(0, D, 2):
                        to = ps[:, i, 2 * P * h:2 * P * h + 2 * P]\
                            .rearrange("p (m d c) -> p d m c", m=2, d=D)[:, d:d + 2, :, :]
                        for dy in range(3):
                            at = W * (H // 2 * h + dy) + d
                            mm = nc.tensor.matmul(to, sh_ln1[:, i, at:at + D * P - D + 1:D],
                                                  w_qk[:, dy, :, :, :].rearrange("p d m c -> p (d m c)"),
                                                  start=(dy == 0), stop=(dy == 2), skip_group_check=True)
                if 1 in halves:
                    mm.then_inc(g_qkt.sem, 1)

            def v_by_head(pair):
                xs = plane(sh_ln1)
                for dy in range(3):
                    for d in range(D):
                        mm = nc.tensor.matmul(ps[C * d:C * d + C, 2, :], w_v[:, dy, :],
                                              xs[:, :, dy:dy + H, d:d + W - D + 1:D],
                                              start=(dy == 0), stop=(dy == 2))
                mm.then_inc(g_v4.sem, 1)

            def gram(pair):
                if not is_first(pair):
                    pe.wait_ge(g_x1.sem, g_x1.done(pair - 1))
                for i in range(2):
                    pe.wait_ge(g_qkt_sb.sem, g_qkt_sb.at(pair, i + 1))
                    t = qk_t[:, i, :].rearrange("p (h m k) -> p h m k", h=2, m=2)
                    for h in range(2):
                        mm = nc.tensor.matmul(ps[:, 3, P * i:P * i + P], t[:, h, 1, :], t[:, h, 0, :],
                                              start=(h == 0), stop=(h == 1))
                mm.then_inc(g_gram.sem, 1)

            def by_head(pair):
                pe.wait_ge(g_score.sem, g_score.at(pair, 2))
                nc.tensor.matmul(ps[:, 3, 2 * P:2 * P + 2 * D], kc[:, K_HEAD:K_HEAD + P], sc_d[:, :],
                                 start=True, stop=True).then_inc(g_rep.sem, 1)

            def attn_out(pair):
                pe.wait_ge(g_score.sem, g_score.done(pair))
                pe.wait_ge(g_v4_sb.sem, g_v4_sb.done(pair))
                for i in range(2):
                    mm = nc.tensor.matmul(ps[:, 3, BLK * i:BLK * i + BLK],
                                          mix[:, i, :, :].rearrange("p j o -> p (j o)"), v4[:, i, :],
                                          start=True, stop=True)
                mm.then_inc(g_y.sem, 1)

            def front_read(pair):
                pe.wait_ge(g_qkt_sb.sem, g_qkt_sb.done(pair))
                pe.wait_ge(g_v4_sb.sem, g_v4_sb.done(pair))
                pe.wait_ge(g_score.sem, g_score.at(pair, 3))

            def gate_info(pair, i):
                xs = plane(sh_ln2)
                planes_ready("ln2", pair)
                pe.wait_ge(g_x1.sem, g_x1.done(pair))
                for h in range(2):
                    for dy in range(3):
                        y = H // 2 * h + dy
                        mm = nc.tensor.matmul(ps[:, GI_BANKS[2 * i + h], :],
                                              w_gi[:, dy, :, :].rearrange("p m o -> p (m o)"),
                                              xs[:, i, y:y + H // 2, 0:W], start=(dy == 0), stop=(dy == 2))
                    mm.then_inc(g_i.sem, 1)

            def reduce_1(pair):
                pe.wait_ge(g_gi.sem, g_gi.done(pair))
                for r in range(R):
                    mm = nc.tensor.matmul(ps[C * r:C * r + C, 1, :], w_r1[:, r // 2, :],
                                          gi[:, :, BLK * (r % 2):BLK * (r % 2) + BLK], start=True, stop=True)
                mm.then_inc(g_r1.sem, 1)

            def conv1(pair, early=False):
                planes_ready("x2", pair)
                if not early:
                    pe.wait_ge(g_t_sb.sem, g_t_sb.before(pair))
                block_conv(sh_x2, conv1_bank(early), lambda dy: w_conv[:, 0, dy, :]).then_inc(g_c1.sem, 1)

            def average_mean(pair, early=False):
                avg = kc[:, K_AVG:K_AVG + P]
                pe.wait_ge(g_in.sem, g_in.at(pair, 2))
                if not early:
                    pe.wait_ge(g_pv_sb.sem, g_pv_sb.before(pair))
                nc.tensor.matmul(ps[:, average_bank(early), 0:2], avg, st[:, :, 0], start=True, stop=True)\
                  .then_inc(g_avg.sem, 1)

            def average_var(pair, early=False):
                avg = kc[:, K_AVG:K_AVG + P]
                pe.wait_ge(g_in.sem, g_in.at(pair, 6))
                nc.tensor.matmul(ps[:, average_bank(early), 2:4], avg, inorm_v[:, I_MOMENT, :], start=True, stop=True)\
                  .then_inc(g_avg.sem, 1)

            def refine_conv(k, bank):
                for i in range(2):
                    for dy in range(3):
                        for r in range(R):
                            mm = nc.tensor.matmul(ps[C * r:C * r + C, bank, BLK * i:BLK * i + BLK],
                                                  w_in[:, i, k, dy, :],
                                                  plane(sh_in)[:, i, RH * r + dy:RH * r + dy + RH, 0:W],
                                                  start=(dy == 0), stop=(dy == 2))
                return mm

            def mask_conv(pair, early=False):
                planes_ready("in", pair)
                pe.wait_ge(g_win.sem, g_win.done(pair))
                refine_conv(1, mask_bank(early)).then_inc(g_mk.sem, 1)

            def conv2(pair, early=False):
                refine_conv(0, conv2_bank(early)).then_inc(g_c2.sem, 1)

            def window_q(pair):
                pe.wait_ge(g_xm.sem, g_xm.done(pair))
                for ia in range(2 * TA):
                    i, a = ia // TA, ia % TA
                    rhs = xm[:, i, 1 + TH * a:1 + TH * a + TH, 1:1 + W]\
                        .rearrange("p y (b x) -> p b y x", x=TW)
                    mm = nc.tensor.matmul(ps[:, 4, P * ia:P * ia + P], w_bd[:, 0, :], rhs, start=True, stop=True)
                mm.then_inc(g_q.sem, 1)

            def window_k(pair):
                pe.wait_ge(g_pv_sb.sem, g_pv_sb.before(pair))
                pe.wait_ge(g_halo.sem, g_halo.done(pair))
                pe.wait_ge(g_in.sem, g_in.done(pair))
                pe.wait_ge(g_th.sem, g_th.done(pair))
                for i in range(2):
                    mm = nc.tensor.matmul(ps[:, 5 + i, 0:(RH + 2) * PW], w_bd[:, 1, :],
                                          xm[:, i, :, :].rearrange("p y x -> p (y x)"), start=True, stop=True)
                mm.then_inc(g_k.sem, 1)

            def window_v(pair, early=False):
                if not early:
                    pe.wait_ge(g_o1.sem, g_o1.done(pair))
                pe.wait_ge(g_q_sb.sem, g_q_sb.done(pair))
                pe.wait_ge(g_xw.sem, g_xw.done(pair))
                for u in range(UNITS):
                    half, t = u % 2, u // 2
                    mm = nc.tensor.matmul(ps[KSLOT * half:KSLOT * half + KEYS, (7, 4)[t // 4],
                                             P * (t % 4):P * (t % 4) + P],
                                          xw[:, u, :], w_bd[:, 2, :], start=True, stop=True)
                mm.then_inc(g_v.sem, 1)

            def window_scores(pair):
                pe.wait_ge(g_q_sb.sem, g_q_sb.done(pair))
                pe.wait_ge(g_k_sb.sem, g_k_sb.done(pair))
                for bank in range(2):
                    nc.tensor.matmul(ps[:, 5 + bank, 0:UPB * KEYS], ident_bf[:, :], win_bf[:, :],
                                     start=True, stop=False, skip_group_check=True)
                    for r in range(0, R, 2):
                        for n in range(UPB):
                            u = UPB * bank + n
                            i, a, b = u // (TA * TB), u // TB % TA, u % TB
                            mm = nc.tensor.matmul(ps[C * r:C * r + 2 * C, 5 + bank, KEYS * n:KEYS * n + KEYS],
                                                  q_bd[:, u, r:r + 2, :].rearrange("p r m -> p (r m)"),
                                                  k_h[:, i, TH * a:TH * a + KH, TW * b:TW * b + KW],
                                                  start=False, stop=(n == UPB - 1), skip_group_check=True)
                    mm.then_inc(g_s.sem, 1)

            def probs_transposed(pair):
                for t in range(UNITS // 2):
                    if t % 4 == 0:
                        pe.wait_ge(g_v_sb.sem, g_v_sb.at(pair, t // 4 + 1))
                        pe.wait_ge(g_sm.sem, g_sm.at(pair, 3 * (t // 4) + 7))
                    mm = nc.tensor.transpose(ps[:, (7, 4)[t // 4], P * (t % 4):P * (t % 4) + P],
                                             prob[:, 2 * t:2 * t + 2, :].rearrange("p u k -> p (u k)"),
                                             kc[:, K_ID:K_ID + P])
                    if t % 4 == 3:
                        mm.then_inc(g_t.sem, 1)

            def window_out(pair):
                alone(pe)
                pe.wait_ge(g_t_sb.sem, g_t_sb.done(pair))
                for r in range(R):
                    o = ps[C * r:C * r + C, 5, :].rearrange("p (i a y b x) -> p i a b y x", i=2, a=TA, b=TB, x=TW)
                    for t in range(UNITS // 2):
                        i, a, b = t // (TA * TB // 2), t // (TB // 2) % TA, 2 * (t % (TB // 2))
                        mm = nc.tensor.matmul(o[:, i, a, b:b + 2, :, :], v_t[:, t, C * r:C * r + C],
                                              p_t[:, R * t + r, :, :].rearrange("p h m -> p (h m)"),
                                              start=True, stop=True)
                mm.then_inc(g_pv.sem, 1)

            def step(pair, norm):
                attn_out(pair + 1)
                conv1(pair)
                qk(pair + 2, 0)
                average_mean(pair)
                qk(pair + 2, 1, (0,))
                average_var(pair)
                qk(pair + 2, 1, (1,))
                gram(pair + 2)
                v_by_head(pair + 2)
                mask_conv(pair)
                by_head(pair + 2)
                conv2(pair)
                front_read(pair + 2)
                window_q(pair)
                window_k(pair)
                window_scores(pair)
                window_v(pair)
                gate_info(pair + 1, 0)
                gate_info(pair + 1, 1)
                probs_transposed(pair)
                reduce_1(pair + 1)
                window_out(pair)

            pe.wait_ge(s_wready, W_QKV)
            qk(0, 0)
            pe.wait_ge(s_fold, 2)
            pe.wait_ge(s_wready, W_QKV + 1)
            qk(0, 1)
            gram(0)
            pe.wait_ge(s_consts, 16)
            by_head(0)
            v_by_head(0)
            attn_out(0)
            qk(1, 0)
            qk(1, 1)
            gram(1)
            v_by_head(1)
            by_head(1)
            front_read(1)
            pe.wait_ge(s_wready, W_ALL)
            pe.wait_ge(s_diag, 16 * (1 + R + 2))
            gate_info(0, 0)
            gate_info(0, 1)
            reduce_1(0)
            pe.wait_ge(s_late, 5)
            with pe.Fori(0, PAIRS - 3) as pair:
                step(pair, True)
            step(PAIRS - 3, False)
            but_last, last = PAIRS - 2, PAIRS - 1
            attn_out(last)
            conv1(but_last)
            average_mean(but_last)
            average_var(but_last)
            mask_conv(but_last)
            conv2(but_last)
            gate_info(last, 0)
            window_q(but_last)
            window_k(but_last)
            gate_info(last, 1)
            reduce_1(last)
            window_scores(but_last)
            conv1(last, True)
            window_v(but_last)
            average_mean(last, True)
            average_var(last, True)
            mask_conv(last, True)
            probs_transposed(but_last)
            window_out(but_last)
            window_q(last)
            window_k(last)
            window_scores(last)
            window_v(last, True)
            conv2(last, True)
            probs_transposed(last)
            window_out(last)


def shape_constants():
    import numpy as np
    p = np.arange(P)
    c = np.zeros((P, K_END), np.float32)
    c[:, K_EQ:K_EQ + C] = p[:, None] % C == np.arange(C)
    c[:, K_HEAD:K_HEAD + P] = (p[:, None] // C == p // C) & (p[:, None] % C // D == p % C // D)
    c[:, K_SELJ:K_SELJ + R] = p[:, None] % D == np.arange(R)
    c[:, K_AVG:K_AVG + P] = (p[:, None] % C == p % C) / R
    c[:, K_ID:K_ID + P] = np.eye(P)
    y, x = p[:, None] % (TH * TW) // TW, p[:, None] % TW
    ky, kx = np.arange(KEYS) // KW, np.arange(KEYS) % KW
    near = (ky >= y) & (ky <= y + 2) & (kx >= x) & (kx <= x + 2)
    c[:, K_WIN:K_END] = np.tile(np.where(near, 0.0, -1e30), (1, UPB))
    return c


def kernel(**inputs):
    import numpy as np
    import concourse.bacc as bacc
    from concourse.bass_utils import run_bass_kernel_spmd

    a = {k: np.asarray(v) for k, v in inputs.items()}
    L0 = {k[8:]: v for k, v in a.items() if k.startswith("L0_conv_")}
    L1 = {k[8:]: v for k, v in a.items() if k.startswith("L1_conv_")}

    def by_partition(v):
        return np.tile(v.reshape(C, 1), (R, 1))

    def spread_row(v):
        return np.tile(v.reshape(1, -1), (P, 1))

    def taps(w):
        return w.transpose(3, 1, 2, 0)

    o_rows = L0["o_w"].reshape(C, C // D, D).transpose(1, 2, 0)
    o_rows = np.tile(np.repeat(o_rows.reshape(C // D, D * C), D, axis=0), (R, 1))
    arrays = {
        "x": a["x"].reshape(PAIRS, 2, C, R, BLK).transpose(0, 3, 2, 1, 4).reshape(PAIRS, P, 2 * BLK),
        "shape_consts": shape_constants(),
        "vectors": np.concatenate(
            [by_partition(L1[k]) for k in ("conv1_b", "conv2_b", "mask_b", "q_b", "k_b", "v_b")]
            + [spread_row(L0["scale"])]
            + [spread_row(L0[k]) for k in ("ln1_g", "ln1_b", "ln2_g", "ln2_b")] + [o_rows], axis=1),
        "w1_qkv": np.concatenate([L0[k].reshape(C, C) for k in ("q1", "k1", "v1")], axis=1),
        "w3_qkv": np.stack([taps(L0[k]) for k in ("q3", "k3", "v3")], axis=2)
                    .transpose(1, 0, 2, 3, 4).reshape(C, 3, 3, 3 * C),
        "w1_gi": np.concatenate([L0[k].reshape(EC, C) for k in ("g1", "i1")], axis=1),
        "w3_gi": np.stack([taps(L0[k]) for k in ("g3", "i3")], axis=2)
                   .transpose(1, 0, 2, 3, 4).reshape(EC, 3, 2, 3 * EC),
        "conv_w": np.stack([taps(L1[k]).reshape(3 * C, 3, C) for k in ("conv1_w", "conv2_w", "mask_w")], axis=1),
        "l1_qkv": np.stack([L1[k].reshape(C, C).T for k in ("q_w", "k_w", "v_w")], axis=1),
        "r1_t": L0["r1"].reshape(C, EC).T,
    }
    nc = bacc.Bacc("TRN2", target_bir_lowering=False, num_devices=1)
    feed, args = {}, []
    for name, v in arrays.items():
        v = np.ascontiguousarray(v)
        feed[f"in_{name}"] = v
        args.append(nc.dram_tensor(f"in_{name}", v.shape, mybir.dt.from_np(v.dtype), kind="ExternalInput").ap())
    args.append(nc.dram_tensor("out_x", (PAIRS, P, 2 * BLK), F32, kind="ExternalOutput").ap())
    build(nc, *args)
    out = run_bass_kernel_spmd(nc, [feed], core_ids=[0]).results[0]["out_x"]
    return out.reshape(PAIRS, R, C, 2, BLK).transpose(0, 3, 2, 1, 4).reshape(B, C, H, W)
```
